# Optimizing a Trainium2 kernel written in Bass

```python
import numpy as np
import jax
import jax.numpy as jnp

def _softmax(x, axis=-1):
    return jax.nn.softmax(x, axis=axis)

def _gelu(x):
    return jax.nn.gelu(x, approximate=True)

def _silu(x):
    return jax.nn.silu(x)

def _sigmoid(x):
    return jax.nn.sigmoid(x)

def _layernorm(x, axis=-1, eps=1e-05):
    m = jnp.mean(x, axis=axis, keepdims=True)
    v = jnp.var(x, axis=axis, keepdims=True)
    return (x - m) / jnp.sqrt(v + eps)

def _scatter_add(tgt, idx, src, axis=0):
    return tgt.at[idx].add(src)

def _segment_sum(src, seg, n):
    return jax.ops.segment_sum(src, seg, n)
kernel_name = 'mk_dlrm_tower_d1_rec_r8_067574'

def setup_inputs(seed: int=0):
    np.random.seed(seed)
    _w = jnp.asarray

    def _rec_inputs():
        import jax
        import jax.numpy as jnp
        _tk = jax.random.key(seed)
        dense_ctx = jax.random.normal(jax.random.fold_in(_tk, 190), (512, 16), jnp.float32)
        ids = jnp.stack([jax.random.randint(jax.random.fold_in(_tk, 200 + f), (512,), 0, v, jnp.int32) for f, v in enumerate([12500, 1000, 125000, 12500, 1250, 1250, 1250, 12500, 12500, 125000, 125000, 1250, 125000, 125000, 125000, 1000, 1000, 1250, 1000, 1250, 1250, 1250, 12500, 12500, 1000, 1000, 12500, 125000, 12500, 12500, 125000, 1000, 125000, 1250, 12500, 12500, 125000, 125000, 1250])], axis=1)
        tbl_0 = 0.05 * jax.random.normal(jax.random.fold_in(_tk, 500 + 0), (12500, 16), jnp.float32)
        tbl_1 = 0.05 * jax.random.normal(jax.random.fold_in(_tk, 500 + 1), (1000, 16), jnp.float32)
        tbl_2 = 0.05 * jax.random.normal(jax.random.fold_in(_tk, 500 + 2), (125000, 16), jnp.float32)
        tbl_3 = 0.05 * jax.random.normal(jax.random.fold_in(_tk, 500 + 3), (12500, 16), jnp.float32)
        tbl_4 = 0.05 * jax.random.normal(jax.random.fold_in(_tk, 500 + 4), (1250, 16), jnp.float32)
        tbl_5 = 0.05 * jax.random.normal(jax.random.fold_in(_tk, 500 + 5), (1250, 16), jnp.float32)
        tbl_6 = 0.05 * jax.random.normal(jax.random.fold_in(_tk, 500 + 6), (1250, 16), jnp.float32)
        tbl_7 = 0.05 * jax.random.normal(jax.random.fold_in(_tk, 500 + 7), (12500, 16), jnp.float32)
        tbl_8 = 0.05 * jax.random.normal(jax.random.fold_in(_tk, 500 + 8), (12500, 16), jnp.float32)
        tbl_9 = 0.05 * jax.random.normal(jax.random.fold_in(_tk, 500 + 9), (125000, 16), jnp.float32)
        tbl_10 = 0.05 * jax.random.normal(jax.random.fold_in(_tk, 500 + 10), (125000, 16), jnp.float32)
        tbl_11 = 0.05 * jax.random.normal(jax.random.fold_in(_tk, 500 + 11), (1250, 16), jnp.float32)
        tbl_12 = 0.05 * jax.random.normal(jax.random.fold_in(_tk, 500 + 12), (125000, 16), jnp.float32)
        tbl_13 = 0.05 * jax.random.normal(jax.random.fold_in(_tk, 500 + 13), (125000, 16), jnp.float32)
        tbl_14 = 0.05 * jax.random.normal(jax.random.fold_in(_tk, 500 + 14), (125000, 16), jnp.float32)
        tbl_15 = 0.05 * jax.random.normal(jax.random.fold_in(_tk, 500 + 15), (1000, 16), jnp.float32)
        tbl_16 = 0.05 * jax.random.normal(jax.random.fold_in(_tk, 500 + 16), (1000, 16), jnp.float32)
        tbl_17 = 0.05 * jax.random.normal(jax.random.fold_in(_tk, 500 + 17), (1250, 16), jnp.float32)
        tbl_18 = 0.05 * jax.random.normal(jax.random.fold_in(_tk, 500 + 18), (1000, 16), jnp.float32)
        tbl_19 = 0.05 * jax.random.normal(jax.random.fold_in(_tk, 500 + 19), (1250, 16), jnp.float32)
        tbl_20 = 0.05 * jax.random.normal(jax.random.fold_in(_tk, 500 + 20), (1250, 16), jnp.float32)
        tbl_21 = 0.05 * jax.random.normal(jax.random.fold_in(_tk, 500 + 21), (1250, 16), jnp.float32)
        tbl_22 = 0.05 * jax.random.normal(jax.random.fold_in(_tk, 500 + 22), (12500, 16), jnp.float32)
        tbl_23 = 0.05 * jax.random.normal(jax.random.fold_in(_tk, 500 + 23), (12500, 16), jnp.float32)
        tbl_24 = 0.05 * jax.random.normal(jax.random.fold_in(_tk, 500 + 24), (1000, 16), jnp.float32)
        tbl_25 = 0.05 * jax.random.normal(jax.random.fold_in(_tk, 500 + 25), (1000, 16), jnp.float32)
        tbl_26 = 0.05 * jax.random.normal(jax.random.fold_in(_tk, 500 + 26), (12500, 16), jnp.float32)
        tbl_27 = 0.05 * jax.random.normal(jax.random.fold_in(_tk, 500 + 27), (125000, 16), jnp.float32)
        tbl_28 = 0.05 * jax.random.normal(jax.random.fold_in(_tk, 500 + 28), (12500, 16), jnp.float32)
        tbl_29 = 0.05 * jax.random.normal(jax.random.fold_in(_tk, 500 + 29), (12500, 16), jnp.float32)
        tbl_30 = 0.05 * jax.random.normal(jax.random.fold_in(_tk, 500 + 30), (125000, 16), jnp.float32)
        tbl_31 = 0.05 * jax.random.normal(jax.random.fold_in(_tk, 500 + 31), (1000, 16), jnp.float32)
        tbl_32 = 0.05 * jax.random.normal(jax.random.fold_in(_tk, 500 + 32), (125000, 16), jnp.float32)
        tbl_33 = 0.05 * jax.random.normal(jax.random.fold_in(_tk, 500 + 33), (1250, 16), jnp.float32)
        tbl_34 = 0.05 * jax.random.normal(jax.random.fold_in(_tk, 500 + 34), (12500, 16), jnp.float32)
        tbl_35 = 0.05 * jax.random.normal(jax.random.fold_in(_tk, 500 + 35), (12500, 16), jnp.float32)
        tbl_36 = 0.05 * jax.random.normal(jax.random.fold_in(_tk, 500 + 36), (125000, 16), jnp.float32)
        tbl_37 = 0.05 * jax.random.normal(jax.random.fold_in(_tk, 500 + 37), (125000, 16), jnp.float32)
        tbl_38 = 0.05 * jax.random.normal(jax.random.fold_in(_tk, 500 + 38), (1250, 16), jnp.float32)
        _rk = jax.random.fold_in(_tk, 7)
        W_top1 = 0.0606339 * jax.random.normal(jax.random.fold_in(_tk, 801), (272, 512), jnp.float32)
        W_top2 = 0.0441942 * jax.random.normal(jax.random.fold_in(_tk, 802), (512, 256), jnp.float32)
        W_top3 = 0.0625 * jax.random.normal(jax.random.fold_in(_tk, 803), (256, 1), jnp.float32)
        b_top1 = jnp.zeros((512,), jnp.float32)
        b_top2 = jnp.zeros((256,), jnp.float32)
        return (dense_ctx, ids, tbl_0, tbl_1, tbl_2, tbl_3, tbl_4, tbl_5, tbl_6, tbl_7, tbl_8, tbl_9, tbl_10, tbl_11, tbl_12, tbl_13, tbl_14, tbl_15, tbl_16, tbl_17, tbl_18, tbl_19, tbl_20, tbl_21, tbl_22, tbl_23, tbl_24, tbl_25, tbl_26, tbl_27, tbl_28, tbl_29, tbl_30, tbl_31, tbl_32, tbl_33, tbl_34, tbl_35, tbl_36, tbl_37, tbl_38, W_top1, b_top1, W_top2, b_top2, W_top3)
    dense_ctx, ids, tbl_0, tbl_1, tbl_2, tbl_3, tbl_4, tbl_5, tbl_6, tbl_7, tbl_8, tbl_9, tbl_10, tbl_11, tbl_12, tbl_13, tbl_14, tbl_15, tbl_16, tbl_17, tbl_18, tbl_19, tbl_20, tbl_21, tbl_22, tbl_23, tbl_24, tbl_25, tbl_26, tbl_27, tbl_28, tbl_29, tbl_30, tbl_31, tbl_32, tbl_33, tbl_34, tbl_35, tbl_36, tbl_37, tbl_38, W_top1, b_top1, W_top2, b_top2, W_top3 = _rec_inputs()

    def _L0_rec_setup():
        import jax, jax.numpy as jnp
        import numpy as np
        LAYER_SIZES = [128, 128, 128]
        F0 = 39
        D = 16
        B = 256
        key = jax.random.key(seed)
        ks = jax.random.split(key, 4)
        field_nums = [F0, LAYER_SIZES[0] // 2, LAYER_SIZES[1] // 2]
        x = jax.random.normal(ks[0], (B, F0, D), dtype=jnp.float32)
        W0 = jax.random.normal(ks[1], (F0 * field_nums[0], LAYER_SIZES[0]), dtype=jnp.float32) * 0.05
        W1 = jax.random.normal(ks[2], (F0 * field_nums[1], LAYER_SIZES[1]), dtype=jnp.float32) * 0.05
        W2 = jax.random.normal(ks[3], (F0 * field_nums[2], LAYER_SIZES[2]), dtype=jnp.float32) * 0.05
        b0 = jnp.zeros((LAYER_SIZES[0],), jnp.float32)
        b1 = jnp.zeros((LAYER_SIZES[1],), jnp.float32)
        b2 = jnp.zeros((LAYER_SIZES[2],), jnp.float32)
        return {'x': x, 'W0': W0, 'W1': W1, 'W2': W2, 'b0': b0, 'b1': b1, 'b2': b2}
    _L0_rec_all = _L0_rec_setup()
    _L0_rec_in = {k: v for k, v in _L0_rec_all.items() if k in ('W0', 'W1', 'W2', 'b0', 'b1', 'b2')}
    del _L0_rec_all
    return {'dense_ctx': dense_ctx, 'ids': ids, 'tbl_0': tbl_0, 'tbl_1': tbl_1, 'tbl_2': tbl_2, 'tbl_3': tbl_3, 'tbl_4': tbl_4, 'tbl_5': tbl_5, 'tbl_6': tbl_6, 'tbl_7': tbl_7, 'tbl_8': tbl_8, 'tbl_9': tbl_9, 'tbl_10': tbl_10, 'tbl_11': tbl_11, 'tbl_12': tbl_12, 'tbl_13': tbl_13, 'tbl_14': tbl_14, 'tbl_15': tbl_15, 'tbl_16': tbl_16, 'tbl_17': tbl_17, 'tbl_18': tbl_18, 'tbl_19': tbl_19, 'tbl_20': tbl_20, 'tbl_21': tbl_21, 'tbl_22': tbl_22, 'tbl_23': tbl_23, 'tbl_24': tbl_24, 'tbl_25': tbl_25, 'tbl_26': tbl_26, 'tbl_27': tbl_27, 'tbl_28': tbl_28, 'tbl_29': tbl_29, 'tbl_30': tbl_30, 'tbl_31': tbl_31, 'tbl_32': tbl_32, 'tbl_33': tbl_33, 'tbl_34': tbl_34, 'tbl_35': tbl_35, 'tbl_36': tbl_36, 'tbl_37': tbl_37, 'tbl_38': tbl_38, 'W_top1': W_top1, 'b_top1': b_top1, 'W_top2': W_top2, 'b_top2': b_top2, 'W_top3': W_top3, 'L0_rec_W0': _L0_rec_in['W0'], 'L0_rec_W1': _L0_rec_in['W1'], 'L0_rec_W2': _L0_rec_in['W2'], 'L0_rec_b0': _L0_rec_in['b0'], 'L0_rec_b1': _L0_rec_in['b1'], 'L0_rec_b2': _L0_rec_in['b2']}

def reference(dense_ctx, ids, tbl_0, tbl_1, tbl_2, tbl_3, tbl_4, tbl_5, tbl_6, tbl_7, tbl_8, tbl_9, tbl_10, tbl_11, tbl_12, tbl_13, tbl_14, tbl_15, tbl_16, tbl_17, tbl_18, tbl_19, tbl_20, tbl_21, tbl_22, tbl_23, tbl_24, tbl_25, tbl_26, tbl_27, tbl_28, tbl_29, tbl_30, tbl_31, tbl_32, tbl_33, tbl_34, tbl_35, tbl_36, tbl_37, tbl_38, W_top1, b_top1, W_top2, b_top2, W_top3, L0_rec_W0, L0_rec_W1, L0_rec_W2, L0_rec_b0, L0_rec_b1, L0_rec_b2):
    import jax
    import jax.numpy as jnp

    def _L0_rec_ref(x, W0, W1, W2, b0, b1, b2):
        import jax, jax.numpy as jnp
        import numpy as np
        LAYER_SIZES = [128, 128, 128]
        F0 = 39
        D = 16
        B = 256
        Ws = [W0, W1, W2]
        bs = [b0, b1, b2]
        h = x
        outs = []
        n_layers = len(LAYER_SIZES)
        for i, S in enumerate(LAYER_SIZES):
            Fk = h.shape[1]
            Wr = Ws[i].reshape(F0, Fk, S)
            out = jax.nn.relu(jnp.einsum('bfd,bgd,fgs->bsd', x, h, Wr) + bs[i][None, :, None])
            if i != n_layers - 1:
                h, direct = (out[:, :S // 2], out[:, S // 2:])
            else:
                direct = out
            outs.append(direct)
        result = jnp.concatenate(outs, axis=1)
        return jnp.sum(result, axis=-1)
    e = jnp.stack([tbl_0[ids[:, 0]], tbl_1[ids[:, 1]], tbl_2[ids[:, 2]], tbl_3[ids[:, 3]], tbl_4[ids[:, 4]], tbl_5[ids[:, 5]], tbl_6[ids[:, 6]], tbl_7[ids[:, 7]], tbl_8[ids[:, 8]], tbl_9[ids[:, 9]], tbl_10[ids[:, 10]], tbl_11[ids[:, 11]], tbl_12[ids[:, 12]], tbl_13[ids[:, 13]], tbl_14[ids[:, 14]], tbl_15[ids[:, 15]], tbl_16[ids[:, 16]], tbl_17[ids[:, 17]], tbl_18[ids[:, 18]], tbl_19[ids[:, 19]], tbl_20[ids[:, 20]], tbl_21[ids[:, 21]], tbl_22[ids[:, 22]], tbl_23[ids[:, 23]], tbl_24[ids[:, 24]], tbl_25[ids[:, 25]], tbl_26[ids[:, 26]], tbl_27[ids[:, 27]], tbl_28[ids[:, 28]], tbl_29[ids[:, 29]], tbl_30[ids[:, 30]], tbl_31[ids[:, 31]], tbl_32[ids[:, 32]], tbl_33[ids[:, 33]], tbl_34[ids[:, 34]], tbl_35[ids[:, 35]], tbl_36[ids[:, 36]], tbl_37[ids[:, 37]], tbl_38[ids[:, 38]]], axis=1)
    z = _L0_rec_ref(e, L0_rec_W0, L0_rec_W1, L0_rec_W2, L0_rec_b0, L0_rec_b1, L0_rec_b2)
    z = z.reshape(z.shape[0], -1)
    h = jnp.concatenate([z, dense_ctx], axis=1)
    h = jnp.maximum(h @ W_top1 + b_top1, 0.0)
    h = jnp.maximum(h @ W_top2 + b_top2, 0.0)
    y = h @ W_top3
    return y

_drawn_inputs = setup_inputs


def setup_inputs(seed=0):
    import zlib

    import numpy as np

    out = dict(_drawn_inputs(seed))
    spreads = {'b_top1': (0.0, 0.8),
     'b_top2': (0.0, 0.8),
     'L0_rec_b0': (0.0, 0.335),
     'L0_rec_b1': (0.0, 0.483),
     'L0_rec_b2': (0.0, 0.282)}
    factors = {'tbl_0': 8.0,
     'tbl_1': 8.0,
     'tbl_2': 8.0,
     'tbl_3': 8.0,
     'tbl_4': 8.0,
     'tbl_5': 8.0,
     'tbl_6': 8.0,
     'tbl_7': 8.0,
     'tbl_8': 8.0,
     'tbl_9': 8.0,
     'tbl_10': 8.0,
     'tbl_11': 8.0,
     'tbl_12': 8.0,
     'tbl_13': 8.0,
     'tbl_14': 8.0,
     'tbl_15': 8.0,
     'tbl_16': 8.0,
     'tbl_17': 8.0,
     'tbl_18': 8.0,
     'tbl_19': 8.0,
     'tbl_20': 8.0,
     'tbl_21': 8.0,
     'tbl_22': 7.436,
     'tbl_23': 8.0,
     'tbl_24': 8.0,
     'tbl_25': 8.0,
     'tbl_26': 8.0,
     'tbl_27': 8.0,
     'tbl_28': 8.0,
     'tbl_29': 8.0,
     'tbl_30': 8.0,
     'tbl_31': 7.584,
     'tbl_32': 8.0,
     'tbl_33': 8.0,
     'tbl_34': 8.0,
     'tbl_35': 8.0,
     'tbl_36': 8.0,
     'tbl_37': 8.0,
     'tbl_38': 8.0,
     'L0_rec_W0': 6.551,
     'L0_rec_W1': 3.28,
     'dense_ctx': 6.376}
    for name, (base, spread) in spreads.items():
        noise = np.random.default_rng([zlib.crc32(name.encode()), seed]).standard_normal(out[name].shape)
        drawn = base * np.exp(spread * noise) if base else spread * noise
        out[name] = jnp.asarray(drawn.astype(out[name].dtype))
    for name, factor in factors.items():
        out[name] = (out[name] * factor).astype(out[name].dtype)
    return out
```

```python
from contextlib import ExitStack

import concourse.bass as bass
from concourse import mybir

ALU = mybir.AluOpType
ACT = mybir.ActivationFunctionType
AX = mybir.AxisListType
F32 = mybir.dt.float32
F32R = mybir.dt.float32r
I32 = mybir.dt.int32

FIELDS = 39
DIM = 16
BATCH = 512
SIZE = 128
HALF = SIZE // 2
VOCAB = [12500, 1000, 125000, 12500, 1250, 1250, 1250, 12500, 12500, 125000, 125000, 1250, 125000,
         125000, 125000, 1000, 1000, 1250, 1000, 1250, 1250, 1250, 12500, 12500, 1000, 1000, 12500,
         125000, 12500, 12500, 125000, 1000, 125000, 1250, 12500, 12500, 125000, 125000, 1250]

COLS = 512
ROWS = COLS // DIM
CHUNKS = BATCH // ROWS
PER = 128 // ROWS
GATHERS = -(-FIELDS // PER)
LAST = (FIELDS - PER * (GATHERS - 1)) * ROWS

SHIFTS = 3
PAIR_ROWS = FIELDS * SHIFTS
TILES0 = 7
MIRRORED = range(1, 19)
ARRANGED = FIELDS + SHIFTS * TILES0 - 1

TILES = -(-FIELDS // 2)
PIECE = 4
PIECES = TILES // PIECE

RING = 3

MODES1 = "VFVFVFVFVF"
MODES0 = "VFVF"
MODES2 = "FVFVFVFVFV"
GROUPS1 = [(1, j, 2, m) for j, m in zip(range(0, TILES, 2), MODES1)]
GROUPS0 = [(0, j, min(2, TILES0 - j), m) for j, m in zip(range(0, TILES0, 2), MODES0)]
GROUPS2 = [(2, j, 2, m) for j, m in zip(range(0, TILES, 2), MODES2)]
GROUPS = GROUPS1 + GROUPS0 + GROUPS2
N1, N0 = len(GROUPS1), len(GROUPS0)
END1, END0 = N1 - 1, N1 + N0 - 1
LAYER0 = range(N1, N1 + N0)
GROUP_ROWS = {0: PAIR_ROWS, 1: 128, 2: 128}


PROLOGUE, FINAL = 0, CHUNKS


def earlier(g, run=None):
    if run == PROLOGUE:
        return GROUPS[N1:g]
    if run == FINAL and g > END0:
        return GROUPS0 + GROUPS[:N1] + GROUPS[END0 + 1:g]
    return GROUPS0 + GROUPS[:g]


def slot(g, run=None):
    return len(earlier(g, run)) % RING


def split_in(modes, groups=GROUPS):
    return sum(m in modes for *_, m in groups)


assert len(GROUPS) % RING == 0


def build(nc, table, ids, bases, dense, w0, w0_mirror, w1, w2, b0, b1, b2, wt1, bt1, wt2, bt2, wt3, out):
    ctx = ExitStack()

    def sb(name, shape, dt=F32):
        return ctx.enter_context(nc.sbuf_tensor(name, shape, dt))

    def ps(name):
        return ctx.enter_context(nc.psum_tensor(name, [128, COLS], F32))

    def sem(name):
        return ctx.enter_context(nc.semaphore(name))

    with ctx:
        x_scratch = nc.dram_tensor("x_scratch", [CHUNKS, ARRANGED + 1, COLS], F32, kind="Internal")

        ids_sb = sb("ids_sb", [128, CHUNKS * GATHERS], I32)
        bases_sb = sb("bases_sb", [128, GATHERS], I32)
        rows_now = sb("rows_now", [128, GATHERS], I32)
        gathered_x = sb("gathered_x", [128, GATHERS, DIM])

        w_raw = {0: sb("w0_raw", [PAIR_ROWS, TILES0, SIZE]), 1: sb("w1_raw", [128, TILES, SIZE]),
                 2: sb("w2_raw", [128, TILES, SIZE])}
        mirror = sb("mirror", [PAIR_ROWS, TILES0, SIZE])
        split_tiles, split_list = {}, []
        for layer, j, n, m in GROUPS0 + GROUPS1 + GROUPS2:
            if m != "F":
                split_list.append((layer, j, n, len(split_tiles)))
                for t in range(j, j + n):
                    split_tiles[layer, t] = len(split_tiles)
        w_hi = sb("w_hi", [128, len(split_tiles), SIZE], F32R)
        w_lo = sb("w_lo", [128, len(split_tiles), SIZE], F32R)
        bias = {0: sb("bias0", [128, 1]), 1: sb("bias1", [128, 1]), 2: sb("bias2", [128, 1])}

        x_pairs = sb("x_pairs", [128, TILES, COLS])
        x_same = sb("x_same", [PAIR_ROWS, COLS])
        x_shifted = sb("x_shifted", [PAIR_ROWS, TILES0, COLS])
        h1 = sb("h1", [128, COLS])
        h2 = sb("h2", [128, COLS])
        direct01 = sb("direct01", [128, COLS])
        direct2 = sb("direct2", [128, COLS])
        z = sb("z", [128, RING, 2, COLS])
        z_hi = sb("z_hi", [128, RING, 2, COLS], F32R)
        z_lo = sb("z_lo", [128, RING, 2, COLS], F32R)

        pooled01 = sb("pooled01", [128, BATCH])
        pooled2 = sb("pooled2", [128, BATCH])
        dense_sb = sb("dense_sb", [DIM, BATCH])
        wt1_sb = sb("wt1_sb", [128, 2, 512])
        wt1_dense = sb("wt1_dense", [DIM, 512])
        wt2_sb = sb("wt2_sb", [128, 4, 256])
        wt3_sb = sb("wt3_sb", [128, 2])
        bt1_sb = sb("bt1_sb", [128, 4])
        bt2_sb = sb("bt2_sb", [128, 2])
        top1 = x_pairs[:, 0:4, :]
        top2 = x_pairs[:, 4:6, :]
        y_sb = sb("y_sb", [128, BATCH // 128])

        acc = {0: ps("acc0"), 1: ps("acc1"), 2: ps("acc2")}
        top_acc = [ps("top_acc0"), ps("top_acc1")]
        y_acc = ps("y_acc")

        ids_loaded = sem("ids_loaded")
        x_gathered = sem("x_gathered")
        scratch_written = sem("scratch_written")
        x_same_loaded = sem("x_same_loaded")
        x_shifted_loaded = sem("x_shifted_loaded")
        x_pairs_loaded = [sem(f"x_pairs_loaded{p}") for p in range(PIECES)]
        w_loaded = {n: sem(f"w{n}_loaded") for n in (0, 1, 2)}
        mirror_loaded = sem("mirror_loaded")
        top_loaded = sem("top_loaded")
        w0_summed = sem("w0_summed")
        w_hi_ready = sem("w_hi_ready")
        w_lo_ready = sem("w_lo_ready")
        mirror_cleared = sem("mirror_cleared")
        w_padded = sem("w_padded")
        z_ready = sem("z_ready")
        z_hi_ready = sem("z_hi_ready")
        z_lo_by_vector = sem("z_lo_by_vector")
        z_lo_by_gpsimd = sem("z_lo_by_gpsimd")
        z_used = sem("z_used")
        h1_ready = sem("h1_ready")
        h2_ready = sem("h2_ready")
        direct0_ready = sem("direct0_ready")
        direct1_ready = sem("direct1_ready")
        direct2_ready = sem("direct2_ready")
        pooled01_ready = sem("pooled01_ready")
        pooled2_ready = sem("pooled2_ready")
        top1_acc_ready = sem("top1_acc_ready")
        top1_ready = sem("top1_ready")
        top2_acc_ready = sem("top2_acc_ready")
        top2_ready = sem("top2_ready")
        y_acc_ready = sem("y_acc_ready")
        y_ready = sem("y_ready")
        out_written = sem("out_written")

        def made(i, g, run=None):
            return i * len(GROUPS) + (len(earlier(g, run)) + 1)

        def split_made(i, g, modes, run=None):
            return i * split_in(modes) + split_in(modes, earlier(g, run) + [GROUPS[g]])


        block = ctx.enter_context(nc.Block())

        @block.sync
        def _(sp):
            def write_scratch(c):
                sp.wait_ge(x_gathered, 16 * GATHERS * (c + 1))
                whole = PER * (GATHERS - 1)
                x_c = x_scratch[c, 0:whole, :].rearrange("(g f) (r d) -> (f r) g d", f=PER, d=DIM)
                sp.dma_start(x_c, gathered_x[:, 0:GATHERS - 1, :]).then_inc(scratch_written, 16)
                x_c = x_scratch[c, whole:FIELDS, :].rearrange("f (r d) -> (f r) d", d=DIM)
                sp.dma_start(x_c, gathered_x[0:LAST, GATHERS - 1, :]).then_inc(scratch_written, 16)
                again = (ARRANGED + 1 - FIELDS) // PER
                x_c = x_scratch[c, FIELDS:FIELDS + again * PER, :].rearrange(
                    "(g f) (r d) -> (f r) g d", f=PER, d=DIM)
                sp.dma_start(x_c, gathered_x[:, 0:again, :]).then_inc(scratch_written, 16)

            def load_layer0(c, written):
                sp.wait_ge(scratch_written, written)
                for k in range(SHIFTS):
                    rows = slice(FIELDS * k, FIELDS * (k + 1))
                    sp.dma_start(x_same[rows, :], x_scratch[c, 0:FIELDS, :]).then_inc(x_same_loaded, 16)
                    first = x_scratch[c, k:k + 1, :]
                    src = bass.AP(first.tensor, first.offset,
                                  [[COLS, FIELDS], [SHIFTS * COLS, TILES0], [1, COLS]])
                    sp.dma_start(x_shifted[rows, :, :], src).then_inc(x_shifted_loaded, 16)

            def load_pairs(c, p):
                for i in range(2):
                    first = x_scratch[c, 2 * PIECE * p + i:2 * PIECE * p + i + 1, :]
                    src = bass.AP(first.tensor, first.offset,
                                  [[0, HALF], [2 * COLS, PIECE], [1, COLS]])
                    sp.dma_start(x_pairs[HALF * i:HALF * (i + 1), PIECE * p:PIECE * (p + 1), :], src)\
                        .then_inc(x_pairs_loaded[p], 16)

            sp.dma_start(ids_sb[:, :], ids).then_inc(ids_loaded, 16)
            sp.dma_start(bases_sb[:, :], bases).then_inc(ids_loaded, 16)
            sp.dma_start(w_raw[0][:, :, :], w0).then_inc(w_loaded[0], 16)
            sp.wait_ge(mirror_cleared, 1)
            for k, t0, t1 in ((0, 1, 7), (1, 0, 6), (2, 0, 6)):
                rows = slice(FIELDS * k, FIELDS * (k + 1))
                sp.dma_start(mirror[rows, t0:t1, :], w0_mirror[rows, t0:t1, :])\
                    .then_inc(mirror_loaded, 16)
            for n, w in ((1, w1), (2, w2)):
                whole = FIELDS // 2
                sp.dma_start(w_raw[n][:, 0:whole, :],
                             w[0:128 * whole, :].rearrange("(t p) s -> p t s", p=128)).then_inc(w_loaded[n], 16)
                sp.dma_start(w_raw[n][0:HALF, whole, :], w[128 * whole:, :]).then_inc(w_loaded[n], 16)
            for n, b in ((0, b0), (1, b1), (2, b2)):
                sp.dma_start(bias[n][:, :], b.rearrange("(p a) -> p a", a=1)).then_inc(w_loaded[n], 16)
            write_scratch(0)
            load_layer0(0, 48)
            for p in range(PIECES):
                load_pairs(0, p)
            sp.dma_start(wt1_sb[:, :, :], wt1[0:256, :].rearrange("(t p) n -> p t n", p=128)).then_inc(top_loaded, 16)
            sp.dma_start(wt1_dense[:, :], wt1[256:, :]).then_inc(top_loaded, 16)
            sp.dma_start(wt2_sb[:, :, :], wt2.rearrange("(t p) n -> p t n", p=128)).then_inc(top_loaded, 16)
            sp.dma_start(wt3_sb[:, :], wt3).then_inc(top_loaded, 16)
            sp.dma_start(bt1_sb[:, :], bt1).then_inc(top_loaded, 16)
            sp.dma_start(bt2_sb[:, :], bt2).then_inc(top_loaded, 16)
            sp.dma_start(dense_sb[:, :], dense).then_inc(top_loaded, 16)
            write_scratch(1)
            sp.wait_ge(z_ready, N0)
            load_layer0(1, 96)

            def iteration(i, ahead):
                if ahead:
                    write_scratch(i + 2)
                    written = sp.snap(i * 48 + 48 * 3)
                    sp.wait_ge(z_ready, made(i, END0))
                    load_layer0(i + 2, written)
                for p in range(PIECES):
                    sp.wait_ge(z_ready, made(i, END0 + PIECE // 2 * (p + 1)))
                    load_pairs(i + 1, p)

            with sp.Fori(0, CHUNKS - 2) as i:
                iteration(i, True)
            iteration(CHUNKS - 2, False)
            sp.wait_ge(y_ready, 1)
            sp.dma_start(out.rearrange("(p t) a -> p (t a)", p=128), y_sb[:, :]).then_inc(out_written, 16)
            sp.wait_ge(out_written, 16)

        @block.gpsimd
        def _(pool):
            def gather(c):
                nc.gpsimd.tensor_tensor(rows_now[:, :], ids_sb[:, bass.ds(c * GATHERS, GATHERS)],
                                        bases_sb[:, :], ALU.add)
                pool.drain()
                for g in range(GATHERS):
                    n = 128 if g < GATHERS - 1 else LAST
                    nc.gpsimd.indirect_dma_start(
                        gathered_x[0:n, g, :], None, table,
                        bass.IndirectOffsetOnAxis(ap=rows_now[0:n, g:g + 1], axis=0)).then_inc(x_gathered, 16)

            def lows(i, groups, run=None):
                for g in groups:
                    layer, _, n, m = GROUPS[g]
                    if m == "G":
                        s = slot(g, run)
                        k = GROUP_ROWS[layer]
                        pool.wait_ge(z_hi_ready, split_made(i, g, "VG", run))
                        nc.gpsimd.tensor_tensor(z_lo[0:k, s, 0:n, :], z[0:k, s, 0:n, :],
                                                z_hi[0:k, s, 0:n, :].bitcast(F32), ALU.subtract)\
                            .then_inc(z_lo_by_gpsimd, 1)

            for n in (1, 2):
                nc.gpsimd.memset(w_raw[n][HALF:, TILES - 1, :], 0.0).then_inc(w_padded, 1)
            pool.wait_ge(w_padded, 2)
            pool.wait_ge(ids_loaded, 32)
            gather(0)
            pool.wait_ge(scratch_written, 48)
            gather(1)
            lows(0, LAYER0, PROLOGUE)
            with pool.Fori(0, CHUNKS - 2) as i:
                pool.wait_ge(scratch_written, i * 48 + 96)
                gather(i + 2)
                lows(i, range(len(GROUPS)))
            lows(CHUNKS - 2, range(len(GROUPS)))
            lows(CHUNKS - 1, [g for g in range(len(GROUPS)) if g not in LAYER0], FINAL)

        @block.vector
        def _(dve):
            def product(i, g, run=None):
                layer, j, n, m = GROUPS[g]
                s = slot(g, run)
                k = GROUP_ROWS[layer]
                if not (isinstance(i, int) and made(i, g, run) <= RING):
                    dve.wait_ge(z_used, made(i, g, run) - RING)
                if layer == 0:
                    if j == 0:
                        loads = i * 16 * SHIFTS + 16 * SHIFTS * (1 if run == PROLOGUE else 2)
                        dve.wait_ge(x_same_loaded, loads)
                        dve.wait_ge(x_shifted_loaded, loads)
                    in0, h = x_shifted[:, j:j + n, :], x_same[:, :]
                else:
                    if j % PIECE == 0:
                        dve.wait_ge(x_pairs_loaded[j // PIECE], i * 32 + 32)
                    if j == 0:
                        dve.wait_ge({1: h1_ready, 2: h2_ready}[layer], i * 2 + 2)
                    in0, h = x_pairs[:, j:j + n, :], {1: h1, 2: h2}[layer][:, :]
                nc.vector.tensor_tensor(z[0:k, s, 0:n, :], in0, h.unsqueeze(1).broadcast_to([k, n, COLS]),
                                        ALU.mult).then_inc(z_ready, 1)

            def low(i, g, run=None):
                layer, _, n, m = GROUPS[g]
                if m != "V":
                    return
                s = slot(g, run)
                k = GROUP_ROWS[layer]
                dve.wait_ge(z_hi_ready, split_made(i, g, "VG", run))
                nc.vector.tensor_tensor(z_lo[0:k, s, 0:n, :], z[0:k, s, 0:n, :],
                                        z_hi[0:k, s, 0:n, :].bitcast(F32), ALU.subtract)\
                    .then_inc(z_lo_by_vector, 1)

            def pool01(i):
                dve.wait_ge(direct0_ready, i + 1)
                dve.wait_ge(direct1_ready, i + 1)
                nc.vector.tensor_reduce(pooled01[:, bass.ds(i * ROWS, ROWS)],
                                        direct01[:, :].rearrange("p (r d) -> p r d", d=DIM),
                                        AX.X, ALU.add).then_inc(pooled01_ready, 1)

            def pool2(i):
                dve.wait_ge(direct2_ready, i + 1)
                nc.vector.tensor_reduce(pooled2[:, bass.ds(i * ROWS, ROWS)],
                                        direct2[:, :].rearrange("p (r d) -> p r d", d=DIM),
                                        AX.X, ALU.add).then_inc(pooled2_ready, 1)

            def iteration(i, run=None, first=False):
                todo = [g for g in range(len(GROUPS)) if not (run == FINAL and g in LAYER0)]
                for n, g in enumerate(todo):
                    product(i, g, run)
                    if n:
                        low(i, todo[n - 1], run)
                    if g == 4 and not first:
                        pool2(i - 1)
                    if g == END0 + 2:
                        pool01(i)
                low(i, todo[-1], run)

            nc.vector.memset(mirror[:, :, :], 0.0).then_inc(mirror_cleared, 1)
            dve.wait_ge(mirror_loaded, 48)
            dve.wait_ge(w_loaded[0], 32)
            nc.vector.tensor_tensor(w_raw[0][:, :, :], w_raw[0][:, :, :], mirror[:, :, :], ALU.add)\
                .then_inc(w0_summed, 1)
            for n, (layer, t, m, q) in enumerate(split_list):
                k = GROUP_ROWS[layer]
                dve.wait_ge(w_hi_ready, n + 1)
                nc.vector.tensor_tensor(w_lo[0:k, q:q + m, :], w_raw[layer][:, t:t + m, :],
                                        w_hi[0:k, q:q + m, :].bitcast(F32), ALU.subtract).then_inc(w_lo_ready, 1)
            for g in LAYER0:
                product(0, g, PROLOGUE)
                if g > LAYER0[0]:
                    low(0, g - 1, PROLOGUE)
            low(0, END0, PROLOGUE)
            iteration(0, first=True)
            with dve.Fori(1, CHUNKS - 1) as i:
                iteration(i)
            iteration(CHUNKS - 1, FINAL)
            pool2(CHUNKS - 1)
            dve.wait_ge(y_acc_ready, 1)
            nc.vector.tensor_copy(y_sb[:, :], y_acc[:, 0:BATCH // 128]).then_inc(y_ready, 1)

        @block.scalar
        def _(act):
            def high(i, g, run=None):
                layer, _, n, m = GROUPS[g]
                if m == "F":
                    return
                s = slot(g, run)
                k = GROUP_ROWS[layer]
                act.wait_ge(z_ready, made(i, g, run))
                nc.scalar.activation(z_hi[0:k, s, 0:n, :], z[0:k, s, 0:n, :], ACT.Copy)\
                    .then_inc(z_hi_ready, 1)

            def relu(dst, layer, p0, done):
                nc.scalar.activation(dst, acc[layer][p0:p0 + HALF, :], ACT.Relu,
                                     bias=bias[layer][p0:p0 + HALF, :]).then_inc(done, 1)

            def finish0(c):
                act.wait_ge(z_used, made(0, END0, PROLOGUE) if isinstance(c, int) and c == 0 else
                            made(c - 1, END0))
                relu(h1[0:HALF, :], 0, 0, h1_ready)
                relu(h1[HALF:, :], 0, 0, h1_ready)

            def finish0_direct(c, first=False):
                if not first:
                    act.wait_ge(pooled01_ready, c)
                relu(direct01[HALF:, :], 0, HALF, direct0_ready)

            def finish1(c):
                act.wait_ge(z_used, made(c, END1))
                relu(h2[HALF:, :], 1, HALF, h2_ready)
                relu(h2[0:HALF, :], 1, HALF, h2_ready)
                relu(direct01[0:HALF, :], 1, 0, direct1_ready)

            def finish2(c, run=None):
                act.wait_ge(z_used, made(c, len(GROUPS) - 1, run))
                nc.scalar.activation(direct2[:, :], acc[2][:, :], ACT.Relu, bias=bias[2][:, :])\
                    .then_inc(direct2_ready, 1)

            def iteration(i, run=None, first=False):
                for g in range(len(GROUPS)):
                    if run == FINAL and g in LAYER0:
                        continue
                    high(i, g, run)
                    if g == 1 and not first:
                        finish2(i - 1)
                    if g == (END1 if run == FINAL else END1 + 2):
                        finish1(i)
                    if g == END0 + 2 and run != FINAL:
                        finish0(i + 1)
                        finish0_direct(i + 1)

            act.wait_ge(w0_summed, 1)
            for n, (layer, t, m, q) in enumerate(split_list):
                k = GROUP_ROWS[layer]
                if layer and split_list[n - 1][0] != layer:
                    act.wait_ge(w_loaded[layer], 48)
                    act.wait_ge(w_padded, layer)
                nc.scalar.activation(w_hi[0:k, q:q + m, :], w_raw[layer][:, t:t + m, :], ACT.Copy)\
                    .then_inc(w_hi_ready, 1)
            for g in LAYER0:
                high(0, g, PROLOGUE)
            finish0(0)
            finish0_direct(0, first=True)
            iteration(0, first=True)
            with act.Fori(1, CHUNKS - 1) as i:
                iteration(i)
            iteration(CHUNKS - 1, FINAL)
            finish2(CHUNKS - 1, FINAL)
            act.wait_ge(top_loaded, 16 * 7)
            for m in range(4):
                act.wait_ge(top1_acc_ready, m + 1)
                nc.scalar.activation(top1[:, m, :], top_acc[m % 2][:, :], ACT.Relu,
                                     bias=bt1_sb[:, m:m + 1]).then_inc(top1_ready, 1)
            for m in range(2):
                act.wait_ge(top2_acc_ready, m + 1)
                nc.scalar.activation(top2[:, m, :], top_acc[m % 2][:, :], ACT.Relu,
                                     bias=bt2_sb[:, m:m + 1]).then_inc(top2_ready, 1)

        @block.tensor
        def _(pe):
            def group(i, g, run=None):
                layer, j, n, m = GROUPS[g]
                s = slot(g, run)
                k = GROUP_ROWS[layer]
                tiles = TILES if layer else TILES0
                if m == "F":
                    pe.wait_ge(z_ready, made(i, g, run))
                else:
                    lo_ready = {"V": z_lo_by_vector, "G": z_lo_by_gpsimd}[m]
                    pe.wait_ge(lo_ready, split_made(i, g, m, run))
                for t in range(j, j + n):
                    if m == "F":
                        parts = [(w_raw[layer][:, t, :], z)]
                    else:
                        q = split_tiles[layer, t]
                        parts = [(w_lo[0:k, q, :], z_hi), (w_hi[0:k, q, :], z_hi), (w_hi[0:k, q, :], z_lo)]
                    for u, (w, of) in enumerate(parts):
                        last = nc.tensor.matmul(acc[layer][:, :], w, of[0:k, s, t - j, :],
                                                start=(t == 0 and u == 0),
                                                stop=(t == tiles - 1 and u == len(parts) - 1))
                last.then_inc(z_used, 1)

            def iteration(i, run=None):
                for g in range(len(GROUPS)):
                    layer = GROUPS[g][0]
                    if run == FINAL and layer == 0:
                        continue
                    if g == N1:
                        pe.wait_ge(h1_ready, i * 2 + 2)
                        pe.wait_ge(direct0_ready, i + 1)
                    group(i, g, run)

            pe.wait_ge(w0_summed, 1)
            pe.wait_ge(w_lo_ready, sum(layer == 0 for layer, *_ in split_list))
            for g in LAYER0:
                group(0, g, PROLOGUE)
            pe.wait_ge(w_loaded[1], 48)
            pe.wait_ge(w_loaded[2], 48)
            pe.wait_ge(w_padded, 2)
            pe.wait_ge(w_lo_ready, len(split_list))
            with pe.Fori(0, CHUNKS - 1) as i:
                iteration(i)
            iteration(CHUNKS - 1, FINAL)
            pe.wait_ge(top_loaded, 16 * 7)
            pe.wait_ge(pooled01_ready, CHUNKS)
            pe.wait_ge(pooled2_ready, CHUNKS)
            for m in range(4):
                if m >= 2:
                    pe.wait_ge(top1_ready, m - 1)
                at = slice(128 * m, 128 * (m + 1))
                a = top_acc[m % 2][:, :]
                nc.tensor.matmul(a, wt1_sb[:, 0, at], pooled01[:, :], start=True, stop=False)
                nc.tensor.matmul(a, wt1_dense[:, at], dense_sb[:, :], start=False, stop=False)
                nc.tensor.matmul(a, wt1_sb[:, 1, at], pooled2[:, :], start=False, stop=True)\
                    .then_inc(top1_acc_ready, 1)
            pe.wait_ge(top1_ready, 4)
            for m in range(2):
                for t in range(4):
                    last = nc.tensor.matmul(top_acc[m][:, :], wt2_sb[:, t, 128 * m:128 * (m + 1)],
                                            top1[:, t, :], start=(t == 0), stop=(t == 3))
                last.then_inc(top2_acc_ready, 1)
            pe.wait_ge(top2_ready, 2)
            four = BATCH // 128
            for t in range(four):
                for m in range(2):
                    last = nc.tensor.matmul(y_acc[:, t:t + 1], top2[:, m, t::four], wt3_sb[:, m:m + 1],
                                            start=(m == 0), stop=(m == 1))
            last.then_inc(y_acc_ready, 1)


def kernel(**inputs):
    import numpy as np
    import concourse.bacc as bacc
    from concourse import mybir as mb
    from concourse.bass_utils import run_bass_kernel_spmd as run

    a = {k: np.asarray(v) for k, v in inputs.items()}
    table = np.concatenate([a[f"tbl_{f}"] for f in range(FIELDS)])
    starts = np.concatenate([[0], np.cumsum(VOCAB)[:-1]]).astype(np.int32)
    padded = np.zeros((BATCH, GATHERS * PER), a["ids"].dtype)
    padded[:, :FIELDS] = a["ids"]
    ids = padded.reshape(CHUNKS, ROWS, GATHERS, PER).transpose(3, 1, 0, 2).reshape(128, CHUNKS * GATHERS)
    bases = np.zeros(GATHERS * PER, np.int32)
    bases[:FIELDS] = starts
    bases = np.repeat(bases.reshape(GATHERS, PER).T, ROWS, axis=0)
    r = a["L0_rec_W0"].reshape(FIELDS, FIELDS, SIZE)
    f = np.arange(FIELDS)[None, :, None]
    s = SHIFTS * np.arange(TILES0)[None, None, :] + np.arange(SHIFTS)[:, None, None]
    other = (f + s) % FIELDS
    w0 = r[f, other].reshape(PAIR_ROWS, TILES0, SIZE)
    w0_mirror = r[other, f].reshape(PAIR_ROWS, TILES0, SIZE)
    swap = np.r_[HALF:SIZE, 0:HALF]
    wt1 = a["W_top1"][np.r_[HALF:SIZE, 0:HALF, SIZE:272]]
    given = {
        "table": table, "ids": ids, "bases": bases, "dense": a["dense_ctx"].T,
        "w0": w0, "w0_mirror": w0_mirror, "w1": a["L0_rec_W1"][:, swap], "w2": a["L0_rec_W2"],
        "b0": a["L0_rec_b0"], "b1": a["L0_rec_b1"][swap], "b2": a["L0_rec_b2"],
        "wt1": wt1, "bt1": a["b_top1"].reshape(4, 128).T, "wt2": a["W_top2"],
        "bt2": a["b_top2"].reshape(2, 128).T, "wt3": a["W_top3"].reshape(2, 128).T,
    }
    nc = bacc.Bacc("TRN2", target_bir_lowering=False, num_devices=1)
    arrays, aps = {}, {}
    for name, x in given.items():
        x = np.ascontiguousarray(x)
        arrays[name + "_dram"] = x
        aps[name] = nc.dram_tensor(name + "_dram", x.shape, mb.dt.from_np(x.dtype), kind="ExternalInput").ap()
    out = nc.dram_tensor("out_dram", (BATCH, 1), mb.dt.float32, kind="ExternalOutput").ap()
    build(nc, **aps, out=out)
    result = run(nc, [arrays], core_ids=[0])
    return result.results[0]["out_dram"]
```

```python
from contextlib import ExitStack

import concourse.bass as bass
from concourse import mybir

ALU = mybir.AluOpType
ACT = mybir.ActivationFunctionType
AX = mybir.AxisListType
F32 = mybir.dt.float32
F32R = mybir.dt.float32r
I32 = mybir.dt.int32

FIELDS = 39
DIM = 16
BATCH = 512
SIZE = 128
HALF = SIZE // 2
VOCAB = [12500, 1000, 125000, 12500, 1250, 1250, 1250, 12500, 12500, 125000, 125000, 1250, 125000,
         125000, 125000, 1000, 1000, 1250, 1000, 1250, 1250, 1250, 12500, 12500, 1000, 1000, 12500,
         125000, 12500, 12500, 125000, 1000, 125000, 1250, 12500, 12500, 125000, 125000, 1250]

COLS = 512
ROWS = COLS // DIM
CHUNKS = BATCH // ROWS
PER = 128 // ROWS
GATHERS = -(-FIELDS // PER)
LAST = (FIELDS - PER * (GATHERS - 1)) * ROWS

SHIFTS = 3
PAIR_ROWS = FIELDS * SHIFTS
TILES0 = 7
PARTS0 = [(0, 2), (2, 4), (4, TILES0)]
MIRRORED = range(1, 19)
ARRANGED = FIELDS + SHIFTS * TILES0 - 1

TILES = -(-FIELDS // 2)
PIECE = 4
PIECES = TILES // PIECE

GATHERS_AT = {4: 1, 7: 1, 10: 6, 17: 1, 20: 1}
RING = 6
SPLIT_RING = 4

MODES1 = "FGFVFGFGFG"
MODES0 = "VFFV"
MODES2 = "FFGFGVFGFG"
GROUPS1 = [(1, j, 2, m) for j, m in zip(range(0, TILES, 2), MODES1)]
GROUPS0 = [(0, j, min(2, TILES0 - j), m) for j, m in zip(range(0, TILES0, 2), MODES0)]
GROUPS2 = [(2, j, 2, m) for j, m in zip(range(0, TILES, 2), MODES2)]
START = [(0, j, n, "F") for _, j, n, _ in GROUPS0]
GROUPS = GROUPS1 + GROUPS0 + GROUPS2
N1, N0 = len(GROUPS1), len(GROUPS0)
END1, END0 = N1 - 1, N1 + N0 - 1
LAYER0 = range(N1, N1 + N0)
GROUP_ROWS = {0: PAIR_ROWS, 1: 128, 2: 128}


PROLOGUE, FINAL = 0, CHUNKS


def earlier(g, run=None):
    if run == PROLOGUE:
        return START[:g - N1]
    if run == FINAL and g > END0:
        return START + GROUPS[:N1] + GROUPS[END0 + 1:g]
    return START + GROUPS[:g]


def group_of(g, run=None):
    return START[g - N1] if run == PROLOGUE else GROUPS[g]


def slot(g, run=None):
    return len(earlier(g, run)) % RING


def split_in(modes, groups=GROUPS):
    return sum(m in modes for *_, m in groups)


TOWER_PARTS = [(0, BATCH - ROWS), (BATCH - ROWS, BATCH)]


def split_slot(g, run=None):
    return split_in("VG", earlier(g, run)) % SPLIT_RING


def last_use(i, g, run=None):
    if isinstance(i, int) and i == 0:
        before = [(n + 1, x) for n, x in enumerate(START + GROUPS[:g])]
    else:
        now = earlier(g, run)[N0:]
        before = [(n + 1 + N0 - len(GROUPS), x) for n, x in enumerate(GROUPS + now)]
    before = [n for n, (*_, m) in before if m in "VG"]
    return before[-SPLIT_RING] if len(before) >= SPLIT_RING else None


AFTER1 = END0
AFTER0 = END0 + RING
AFTER2 = RING - 1
assert sum(GATHERS_AT.values()) == GATHERS
assert len(GROUPS) % RING == 0 and split_in("VG") % SPLIT_RING == 0


def build(nc, table, ids, bases, dense, w0, w0_mirror, w1, w2, b0, b1, b2, wt1, bt1, wt2, bt2, wt3, out):
    ctx = ExitStack()

    def sb(name, shape, dt=F32):
        return ctx.enter_context(nc.sbuf_tensor(name, shape, dt))

    def ps(name):
        return ctx.enter_context(nc.psum_tensor(name, [128, COLS], F32))

    def sem(name):
        return ctx.enter_context(nc.semaphore(name))

    with ctx:
        x_scratch = nc.dram_tensor("x_scratch", [CHUNKS, ARRANGED + 1, COLS], F32, kind="Internal")

        ids_sb = sb("ids_sb", [128, CHUNKS * GATHERS], I32)
        bases_sb = sb("bases_sb", [128, GATHERS], I32)
        rows_now = sb("rows_now", [128, GATHERS], I32)
        gathered_x = sb("gathered_x", [128, GATHERS, DIM])

        w_raw = {0: sb("w0_raw", [PAIR_ROWS, TILES0, SIZE]), 1: sb("w1_raw", [128, TILES, SIZE]),
                 2: sb("w2_raw", [128, TILES, SIZE])}
        mirror = sb("mirror", [PAIR_ROWS, TILES0, SIZE])
        split_tiles, split_list = {}, []
        for layer, j, n, m in GROUPS0 + GROUPS1 + GROUPS2:
            if m != "F":
                split_list.append((layer, j, n, len(split_tiles)))
                for t in range(j, j + n):
                    split_tiles[layer, t] = len(split_tiles)
        w_hi = sb("w_hi", [128, len(split_tiles), SIZE], F32R)
        w_lo = sb("w_lo", [128, len(split_tiles), SIZE], F32R)
        bias = {0: sb("bias0", [128, 1]), 1: sb("bias1", [128, 1]), 2: sb("bias2", [128, 1])}

        x_pairs = sb("x_pairs", [128, TILES, COLS])
        x_same_in = sb("x_same_in", [PAIR_ROWS, COLS])
        x_shifted = sb("x_shifted", [128, TILES0, COLS])
        direct01 = sb("direct01", [128, COLS])
        direct2 = sb("direct2", [128, COLS])
        z = sb("z", [128, RING, 2, COLS])
        z_hi = sb("z_hi", [128, SPLIT_RING, 2, COLS], F32R)
        z_lo = sb("z_lo", [128, SPLIT_RING, 2, COLS], F32R)

        pooled01 = sb("pooled01", [128, BATCH])
        pooled2 = sb("pooled2", [128, BATCH])
        dense_sb = sb("dense_sb", [DIM, BATCH])
        wt1_sb = sb("wt1_sb", [128, 2, 512])
        wt1_dense = sb("wt1_dense", [DIM, 512])
        wt2_sb = sb("wt2_sb", [128, 4, 256])
        wt3_sb = sb("wt3_sb", [128, 2])
        bt1_sb = sb("bt1_sb", [128, 4])
        bt2_sb = sb("bt2_sb", [128, 2])
        top1 = x_shifted[:, 0:4, :]
        top2 = x_shifted[:, 4:6, :]
        y_sb = sb("y_sb", [1, BATCH])

        acc = {0: ps("acc0"), 1: ps("acc1"), 2: ps("acc2")}
        top_acc = [ps("top_acc0"), ps("top_acc1")]
        y_acc = acc[0][0:1, :]
        x_same = ps("x_same")
        h1 = ps("h1")
        h2 = ps("h2")

        ids_loaded = sem("ids_loaded")
        x_gathered = sem("x_gathered")
        scratch_written = sem("scratch_written")
        x_same_loaded = sem("x_same_loaded")
        x_same_ready = sem("x_same_ready")
        x_shifted_loaded = [sem(f"x_shifted_loaded{p}") for p in range(len(PARTS0))]
        x_pairs_loaded = [sem(f"x_pairs_loaded{p}") for p in range(PIECES)]
        w_loaded = {n: sem(f"w{n}_loaded") for n in (0, 1, 2)}
        mirror_loaded = sem("mirror_loaded")
        top_loaded = sem("top_loaded")
        w0_summed = sem("w0_summed")
        w_hi_ready = sem("w_hi_ready")
        w_lo_ready = sem("w_lo_ready")
        mirror_cleared = sem("mirror_cleared")
        w_padded = sem("w_padded")
        z_ready = sem("z_ready")
        z_hi_ready = sem("z_hi_ready")
        z_lo_by_vector = sem("z_lo_by_vector")
        z_lo_by_gpsimd = sem("z_lo_by_gpsimd")
        z_used = sem("z_used")
        h1_ready = sem("h1_ready")
        h2_ready = sem("h2_ready")
        direct0_ready = sem("direct0_ready")
        direct1_ready = sem("direct1_ready")
        direct2_ready = sem("direct2_ready")
        pooled01_ready = sem("pooled01_ready")
        pooled2_ready = sem("pooled2_ready")
        top1_acc_ready = sem("top1_acc_ready")
        top1_ready = sem("top1_ready")
        top2_acc_ready = sem("top2_acc_ready")
        top2_ready = sem("top2_ready")
        y_acc_ready = sem("y_acc_ready")
        y_ready = sem("y_ready")
        out_written = sem("out_written")

        def made(i, g, run=None):
            return i * len(GROUPS) + (len(earlier(g, run)) + 1)

        def split_made(i, g, modes, run=None):
            return i * split_in(modes) + split_in(modes, earlier(g, run) + [GROUPS[g]])


        block = ctx.enter_context(nc.Block())

        @block.sync
        def _(sp):
            def write_scratch(c):
                sp.wait_ge(x_gathered, 16 * GATHERS * (c + 1))
                whole = PER * (GATHERS - 1)
                x_c = x_scratch[c, 0:whole, :].rearrange("(g f) (r d) -> (f r) g d", f=PER, d=DIM)
                sp.dma_start(x_c, gathered_x[:, 0:GATHERS - 1, :]).then_inc(scratch_written, 16)
                x_c = x_scratch[c, whole:FIELDS, :].rearrange("f (r d) -> (f r) d", d=DIM)
                sp.dma_start(x_c, gathered_x[0:LAST, GATHERS - 1, :]).then_inc(scratch_written, 16)
                again = (ARRANGED + 1 - FIELDS) // PER
                x_c = x_scratch[c, FIELDS:FIELDS + again * PER, :].rearrange(
                    "(g f) (r d) -> (f r) g d", f=PER, d=DIM)
                sp.dma_start(x_c, gathered_x[:, 0:again, :]).then_inc(scratch_written, 16)

            def load_layer0(c, written):
                sp.wait_ge(scratch_written, written)
                for k in range(SHIFTS):
                    rows = slice(FIELDS * k, FIELDS * (k + 1))
                    sp.dma_start(x_same_in[rows, :], x_scratch[c, 0:FIELDS, :]).then_inc(x_same_loaded, 16)
                for part, (t0, t1) in enumerate(PARTS0):
                    for k in range(SHIFTS):
                        rows = slice(FIELDS * k, FIELDS * (k + 1))
                        first = x_scratch[c, SHIFTS * t0 + k:SHIFTS * t0 + k + 1, :]
                        src = bass.AP(first.tensor, first.offset,
                                      [[COLS, FIELDS], [SHIFTS * COLS, t1 - t0], [1, COLS]])
                        sp.dma_start(x_shifted[rows, t0:t1, :], src).then_inc(x_shifted_loaded[part], 16)

            def load_pairs(c, p):
                for i in range(2):
                    first = x_scratch[c, 2 * PIECE * p + i:2 * PIECE * p + i + 1, :]
                    src = bass.AP(first.tensor, first.offset,
                                  [[0, HALF], [2 * COLS, PIECE], [1, COLS]])
                    sp.dma_start(x_pairs[HALF * i:HALF * (i + 1), PIECE * p:PIECE * (p + 1), :], src)\
                        .then_inc(x_pairs_loaded[p], 16)

            sp.dma_start(ids_sb[:, :], ids).then_inc(ids_loaded, 16)
            sp.dma_start(bases_sb[:, :], bases).then_inc(ids_loaded, 16)
            write_scratch(0)
            load_layer0(0, 48)
            for p in range(PIECES):
                load_pairs(0, p)
            write_scratch(1)
            sp.wait_ge(z_ready, N0)
            load_layer0(1, 96)

            def iteration(i, ahead):
                for p in range(PIECES):
                    sp.wait_ge(z_ready, made(i, END0 + PIECE // 2 * (p + 1)))
                    load_pairs(i + 1, p)
                if ahead:
                    write_scratch(i + 2)
                    load_layer0(i + 2, i * 48 + 48 * 3)

            with sp.Fori(0, CHUNKS - 2) as i:
                iteration(i, True)
            iteration(CHUNKS - 2, False)
            sp.wait_ge(y_ready, 1)
            sp.dma_start(out.rearrange("b a -> a b"), y_sb[:, :]).then_inc(out_written, 16)
            sp.wait_ge(out_written, 16)

        @block.gpsimd
        def _(pool):
            def find_rows(c):
                nc.gpsimd.tensor_tensor(rows_now[:, :], ids_sb[:, bass.ds(c * GATHERS, GATHERS)],
                                        bases_sb[:, :], ALU.add)
                pool.drain()

            def gather(g):
                n = 128 if g < GATHERS - 1 else LAST
                nc.gpsimd.indirect_dma_start(
                    gathered_x[0:n, g, :], None, table,
                    bass.IndirectOffsetOnAxis(ap=rows_now[0:n, g:g + 1], axis=0)).then_inc(x_gathered, 16)

            def low(i, g, run=None):
                layer, _, n, _ = GROUPS[g]
                s, q = slot(g, run), split_slot(g, run)
                k = GROUP_ROWS[layer]
                pool.wait_ge(z_hi_ready, split_made(i, g, "VG", run))
                nc.gpsimd.tensor_tensor(z_lo[0:k, q, 0:n, :], z[0:k, s, 0:n, :],
                                        z_hi[0:k, q, 0:n, :].bitcast(F32), ALU.subtract)\
                    .then_inc(z_lo_by_gpsimd, 1)

            mine = [g for g in range(len(GROUPS)) if GROUPS[g][3] == "G"]

            for n in (1, 2):
                nc.gpsimd.memset(w_raw[n][HALF:, TILES - 1, :], 0.0).then_inc(w_padded, 1)
            pool.wait_ge(w_padded, 2)
            pool.wait_ge(ids_loaded, 32)
            find_rows(0)
            for g in range(GATHERS):
                gather(g)
            pool.wait_ge(scratch_written, 48)
            find_rows(1)
            for g in range(GATHERS):
                gather(g)
            with pool.Fori(0, CHUNKS - 2) as i:
                done = 0
                for g in range(len(GROUPS)):
                    if g in GATHERS_AT:
                        if not done:
                            pool.wait_ge(scratch_written, i * 48 + 96)
                            find_rows(i + 2)
                        for n in range(done, done + GATHERS_AT[g]):
                            gather(n)
                        done += GATHERS_AT[g]
                    if g in mine:
                        low(i, g)
            for g in mine:
                low(CHUNKS - 2, g)
            for g in mine:
                if g not in LAYER0:
                    low(CHUNKS - 1, g, FINAL)

        @block.vector
        def _(dve):
            def product(i, g, run=None):
                layer, j, n, m = group_of(g, run)
                s = slot(g, run)
                k = GROUP_ROWS[layer]
                if not (isinstance(i, int) and made(i, g, run) <= RING):
                    dve.wait_ge(z_used, made(i, g, run) - RING)
                if layer == 0:
                    loads = i * 16 * SHIFTS + 16 * SHIFTS * (1 if run == PROLOGUE else 2)
                    if j == 0:
                        dve.wait_ge(x_same_ready, i + (1 if run == PROLOGUE else 2))
                    for part, (t0, _) in enumerate(PARTS0):
                        if j == t0:
                            dve.wait_ge(x_shifted_loaded[part], loads)
                    in0, h = x_shifted[0:k, j:j + n, :], x_same[0:k, :]
                else:
                    if j % PIECE == 0:
                        dve.wait_ge(x_pairs_loaded[j // PIECE], i * 32 + 32)
                    if j == 0:
                        dve.wait_ge({1: h1_ready, 2: h2_ready}[layer], i * 2 + 2)
                    in0, h = x_pairs[:, j:j + n, :], {1: h1, 2: h2}[layer][:, :]
                nc.vector.tensor_tensor(z[0:k, s, 0:n, :], in0, h.unsqueeze(1).broadcast_to([k, n, COLS]),
                                        ALU.mult).then_inc(z_ready, 1)

            def low(i, g, run=None):
                layer, _, n, m = GROUPS[g]
                if m != "V":
                    return
                s, q = slot(g, run), split_slot(g, run)
                k = GROUP_ROWS[layer]
                dve.wait_ge(z_hi_ready, split_made(i, g, "VG", run))
                nc.vector.tensor_tensor(z_lo[0:k, q, 0:n, :], z[0:k, s, 0:n, :],
                                        z_hi[0:k, q, 0:n, :].bitcast(F32), ALU.subtract)\
                    .then_inc(z_lo_by_vector, 1)

            def pool01(i):
                dve.wait_ge(direct0_ready, i + 1)
                dve.wait_ge(direct1_ready, i + 1)
                nc.vector.tensor_reduce(pooled01[:, bass.ds(i * ROWS, ROWS)],
                                        direct01[:, :].rearrange("p (r d) -> p r d", d=DIM),
                                        AX.X, ALU.add).then_inc(pooled01_ready, 1)

            def pool2(i):
                dve.wait_ge(direct2_ready, i + 1)
                nc.vector.tensor_reduce(pooled2[:, bass.ds(i * ROWS, ROWS)],
                                        direct2[:, :].rearrange("p (r d) -> p r d", d=DIM),
                                        AX.X, ALU.add).then_inc(pooled2_ready, 1)

            def iteration(i, run=None, first=False):
                todo = [g for g in range(len(GROUPS)) if not (run == FINAL and g in LAYER0)]
                for n, g in enumerate(todo):
                    early = run == FINAL and g == END0 + 1
                    if early:
                        low(i, END1, run)
                    product(i, g, run)
                    if n and not early:
                        low(i, todo[n - 1], run)
                    if g == AFTER2 + 2 and not first:
                        pool2(i - 1)
                    if g == END0 + 4:
                        pool01(i)
                low(i, todo[-1], run)

            nc.vector.memset(mirror[:, :, :], 0.0).then_inc(mirror_cleared, 1)
            dve.wait_ge(mirror_loaded, 48)
            dve.wait_ge(w_loaded[0], 32)
            nc.vector.tensor_tensor(w_raw[0][:, :, :], w_raw[0][:, :, :], mirror[:, :, :], ALU.add)\
                .then_inc(w0_summed, 1)
            for n, (layer, t, m, q) in enumerate(split_list):
                k = GROUP_ROWS[layer]
                dve.wait_ge(w_hi_ready, n + 1)
                nc.vector.tensor_tensor(w_lo[0:k, q:q + m, :], w_raw[layer][:, t:t + m, :],
                                        w_hi[0:k, q:q + m, :].bitcast(F32), ALU.subtract).then_inc(w_lo_ready, 1)
            for g in LAYER0:
                product(0, g, PROLOGUE)
            iteration(0, first=True)
            with dve.Fori(1, CHUNKS - 1) as i:
                iteration(i)
            iteration(CHUNKS - 1, FINAL)
            pool2(CHUNKS - 1)
            dve.wait_ge(y_acc_ready, len(TOWER_PARTS))
            nc.vector.tensor_copy(y_sb[:, :], y_acc).then_inc(y_ready, 1)

        @block.scalar
        def _(act):
            def high(i, g, run=None):
                layer, _, n, m = GROUPS[g]
                if m == "F":
                    return
                s, q = slot(g, run), split_slot(g, run)
                k = GROUP_ROWS[layer]
                if last_use(i, g, run) is not None:
                    act.wait_ge(z_used, i * len(GROUPS) + last_use(i, g, run))
                act.wait_ge(z_ready, made(i, g, run))
                nc.scalar.activation(z_hi[0:k, q, 0:n, :], z[0:k, s, 0:n, :], ACT.Copy)\
                    .then_inc(z_hi_ready, 1)

            def place_same(n):
                act.wait_ge(x_same_loaded, n * 16 * SHIFTS + 16 * SHIFTS)
                nc.scalar.activation(x_same[0:PAIR_ROWS, :], x_same_in[:, :], ACT.Copy).then_inc(x_same_ready, 1)

            def relu(dst, layer, p0, done):
                nc.scalar.activation(dst, acc[layer][p0:p0 + HALF, :], ACT.Relu,
                                     bias=bias[layer][p0:p0 + HALF, :]).then_inc(done, 1)

            def finish0(c):
                act.wait_ge(z_used, made(0, END0, PROLOGUE) if isinstance(c, int) and c == 0 else
                            made(c - 1, END0))
                relu(h1[0:HALF, :], 0, 0, h1_ready)
                relu(h1[HALF:, :], 0, 0, h1_ready)

            def finish0_direct(c, first=False):
                if not first:
                    act.wait_ge(pooled01_ready, c)
                relu(direct01[HALF:, :], 0, HALF, direct0_ready)

            def finish1(c):
                act.wait_ge(z_used, made(c, END1))
                relu(h2[HALF:, :], 1, HALF, h2_ready)
                relu(h2[0:HALF, :], 1, HALF, h2_ready)
                relu(direct01[0:HALF, :], 1, 0, direct1_ready)

            def finish2(c, run=None):
                act.wait_ge(z_used, made(c, len(GROUPS) - 1, run))
                nc.scalar.activation(direct2[:, :], acc[2][:, :], ACT.Relu, bias=bias[2][:, :])\
                    .then_inc(direct2_ready, 1)

            def tower_relus(part):
                b0, b1 = TOWER_PARTS[part]
                for m in range(4):
                    act.wait_ge(top1_acc_ready, 4 * part + m + 1)
                    nc.scalar.activation(top1[:, m, b0:b1], top_acc[m % 2][:, b0:b1], ACT.Relu,
                                         bias=bt1_sb[:, m:m + 1]).then_inc(top1_ready, 1)
                for m in range(2):
                    act.wait_ge(top2_acc_ready, 2 * part + m + 1)
                    nc.scalar.activation(top2[:, m, b0:b1], top_acc[m % 2][:, b0:b1], ACT.Relu,
                                         bias=bt2_sb[:, m:m + 1]).then_inc(top2_ready, 1)

            def iteration(i, run=None, first=False):
                for g in range(len(GROUPS)):
                    if run == FINAL and g in LAYER0:
                        continue
                    high(i, g, run)
                    if g == AFTER2 and not first:
                        finish2(i - 1)
                    if g == 5 and run != FINAL:
                        place_same(i + 1)
                    if g == (END1 if run == FINAL else AFTER1):
                        finish1(i)
                        if run == FINAL:
                            act.wait_ge(top_loaded, 16 * 7)
                            tower_relus(0)
                    if g == AFTER0 and run != FINAL:
                        finish0(i + 1)
                        finish0_direct(i + 1)

            act.dma_start(w_raw[0][:, :, :], w0).then_inc(w_loaded[0], 16)
            act.wait_ge(mirror_cleared, 1)
            for k, t0, t1 in ((0, 1, 7), (1, 0, 6), (2, 0, 6)):
                rows = slice(FIELDS * k, FIELDS * (k + 1))
                act.dma_start(mirror[rows, t0:t1, :], w0_mirror[rows, t0:t1, :])\
                    .then_inc(mirror_loaded, 16)
            for n, b in ((0, b0), (1, b1), (2, b2)):
                act.dma_start(bias[n][:, :], b.rearrange("(p a) -> p a", a=1)).then_inc(w_loaded[n], 16)
            for n, w in ((1, w1), (2, w2)):
                whole = FIELDS // 2
                act.dma_start(w_raw[n][:, 0:whole, :],
                              w[0:128 * whole, :].rearrange("(t p) s -> p t s", p=128)).then_inc(w_loaded[n], 16)
                act.dma_start(w_raw[n][0:HALF, whole, :], w[128 * whole:, :]).then_inc(w_loaded[n], 16)
            act.dma_start(wt1_sb[:, :, :], wt1[0:256, :].rearrange("(t p) n -> p t n", p=128)).then_inc(top_loaded, 16)
            act.dma_start(wt1_dense[:, :], wt1[256:, :]).then_inc(top_loaded, 16)
            act.dma_start(wt2_sb[:, :, :], wt2.rearrange("(t p) n -> p t n", p=128)).then_inc(top_loaded, 16)
            act.dma_start(wt3_sb[:, :], wt3).then_inc(top_loaded, 16)
            act.dma_start(bt1_sb[:, :], bt1).then_inc(top_loaded, 16)
            act.dma_start(bt2_sb[:, :], bt2).then_inc(top_loaded, 16)
            act.dma_start(dense_sb[:, :], dense).then_inc(top_loaded, 16)
            act.wait_ge(w0_summed, 1)
            for n, (layer, t, m, q) in enumerate(split_list):
                k = GROUP_ROWS[layer]
                if layer and split_list[n - 1][0] != layer:
                    act.wait_ge(w_loaded[layer], 48)
                    act.wait_ge(w_padded, layer)
                nc.scalar.activation(w_hi[0:k, q:q + m, :], w_raw[layer][:, t:t + m, :], ACT.Copy)\
                    .then_inc(w_hi_ready, 1)
            place_same(0)
            finish0(0)
            finish0_direct(0, first=True)
            iteration(0, first=True)
            with act.Fori(1, CHUNKS - 1) as i:
                iteration(i)
            iteration(CHUNKS - 1, FINAL)
            finish2(CHUNKS - 1, FINAL)
            tower_relus(1)

        @block.tensor
        def _(pe):
            def group(i, g, run=None):
                layer, j, n, m = group_of(g, run)
                s = slot(g, run)
                k = GROUP_ROWS[layer]
                tiles = TILES if layer else TILES0
                if m == "F":
                    pe.wait_ge(z_ready, made(i, g, run))
                else:
                    lo_ready = {"V": z_lo_by_vector, "G": z_lo_by_gpsimd}[m]
                    pe.wait_ge(lo_ready, split_made(i, g, m, run))
                for t in range(j, j + n):
                    if m == "F":
                        parts = [(w_raw[layer][:, t, :], z[0:k, s, t - j, :])]
                    else:
                        q, r = split_tiles[layer, t], split_slot(g, run)
                        hi, lo = z_hi[0:k, r, t - j, :], z_lo[0:k, r, t - j, :]
                        parts = [(w_lo[0:k, q, :], hi), (w_hi[0:k, q, :], hi), (w_hi[0:k, q, :], lo)]
                    for u, (w, of) in enumerate(parts):
                        last = nc.tensor.matmul(acc[layer][:, :], w, of,
                                                start=(t == 0 and u == 0),
                                                stop=(t == tiles - 1 and u == len(parts) - 1))
                last.then_inc(z_used, 1)

            def tower(part):
                b0, b1 = TOWER_PARTS[part]
                pe.wait_ge(top_loaded, 16 * 7)
                pe.wait_ge(pooled01_ready, b1 // ROWS)
                pe.wait_ge(pooled2_ready, b1 // ROWS)
                for m in range(4):
                    if m >= 2:
                        pe.wait_ge(top1_ready, 4 * part + m - 1)
                    elif part:
                        pe.wait_ge(top2_ready, 2 * part)
                    at = slice(128 * m, 128 * (m + 1))
                    a = top_acc[m % 2][:, b0:b1]
                    nc.tensor.matmul(a, wt1_sb[:, 0, at], pooled01[:, b0:b1], start=True, stop=False)
                    nc.tensor.matmul(a, wt1_dense[:, at], dense_sb[:, b0:b1], start=False, stop=False)
                    nc.tensor.matmul(a, wt1_sb[:, 1, at], pooled2[:, b0:b1], start=False, stop=True)\
                        .then_inc(top1_acc_ready, 1)
                pe.wait_ge(top1_ready, 4 * part + 4)
                for m in range(2):
                    for t in range(4):
                        last = nc.tensor.matmul(top_acc[m][:, b0:b1], wt2_sb[:, t, 128 * m:128 * (m + 1)],
                                                top1[:, t, b0:b1], start=(t == 0), stop=(t == 3))
                    last.then_inc(top2_acc_ready, 1)
                for m in range(2):
                    pe.wait_ge(top2_ready, 2 * part + m + 1)
                    last = nc.tensor.matmul(y_acc[:, b0:b1], wt3_sb[:, m:m + 1], top2[:, m, b0:b1],
                                            start=(m == 0), stop=(m == 1))
                last.then_inc(y_acc_ready, 1)

            def iteration(i, run=None):
                for g in range(len(GROUPS)):
                    layer = GROUPS[g][0]
                    if run == FINAL and g == END0 + 1:
                        tower(0)
                    if run == FINAL and layer == 0:
                        continue
                    if g == N1:
                        pe.wait_ge(h1_ready, i * 2 + 2)
                        pe.wait_ge(direct0_ready, i + 1)
                    group(i, g, run)

            pe.wait_ge(w0_summed, 1)
            pe.wait_ge(w_lo_ready, sum(layer == 0 for layer, *_ in split_list))
            for g in LAYER0:
                group(0, g, PROLOGUE)
            pe.wait_ge(w_loaded[1], 48)
            pe.wait_ge(w_loaded[2], 48)
            pe.wait_ge(w_padded, 2)
            pe.wait_ge(w_lo_ready, len(split_list))
            with pe.Fori(0, CHUNKS - 1) as i:
                iteration(i)
            iteration(CHUNKS - 1, FINAL)
            tower(1)


def kernel(**inputs):
    import numpy as np
    import concourse.bacc as bacc
    from concourse import mybir as mb
    from concourse.bass_utils import run_bass_kernel_spmd as run

    a = {k: np.asarray(v) for k, v in inputs.items()}
    table = np.concatenate([a[f"tbl_{f}"] for f in range(FIELDS)])
    starts = np.concatenate([[0], np.cumsum(VOCAB)[:-1]]).astype(np.int32)
    padded = np.zeros((BATCH, GATHERS * PER), a["ids"].dtype)
    padded[:, :FIELDS] = a["ids"]
    ids = padded.reshape(CHUNKS, ROWS, GATHERS, PER).transpose(3, 1, 0, 2).reshape(128, CHUNKS * GATHERS)
    bases = np.zeros(GATHERS * PER, np.int32)
    bases[:FIELDS] = starts
    bases = np.repeat(bases.reshape(GATHERS, PER).T, ROWS, axis=0)
    r = a["L0_rec_W0"].reshape(FIELDS, FIELDS, SIZE)
    f = np.arange(FIELDS)[None, :, None]
    s = SHIFTS * np.arange(TILES0)[None, None, :] + np.arange(SHIFTS)[:, None, None]
    other = (f + s) % FIELDS
    w0 = r[f, other].reshape(PAIR_ROWS, TILES0, SIZE)
    w0_mirror = r[other, f].reshape(PAIR_ROWS, TILES0, SIZE)
    swap = np.r_[HALF:SIZE, 0:HALF]
    wt1 = a["W_top1"][np.r_[HALF:SIZE, 0:HALF, SIZE:272]]
    given = {
        "table": table, "ids": ids, "bases": bases, "dense": a["dense_ctx"].T,
        "w0": w0, "w0_mirror": w0_mirror, "w1": a["L0_rec_W1"][:, swap], "w2": a["L0_rec_W2"],
        "b0": a["L0_rec_b0"], "b1": a["L0_rec_b1"][swap], "b2": a["L0_rec_b2"],
        "wt1": wt1, "bt1": a["b_top1"].reshape(4, 128).T, "wt2": a["W_top2"],
        "bt2": a["b_top2"].reshape(2, 128).T, "wt3": a["W_top3"].reshape(2, 128).T,
    }
    nc = bacc.Bacc("TRN2", target_bir_lowering=False, num_devices=1)
    arrays, aps = {}, {}
    for name, x in given.items():
        x = np.ascontiguousarray(x)
        arrays[name + "_dram"] = x
        aps[name] = nc.dram_tensor(name + "_dram", x.shape, mb.dt.from_np(x.dtype), kind="ExternalInput").ap()
    out = nc.dram_tensor("out_dram", (BATCH, 1), mb.dt.float32, kind="ExternalOutput").ap()
    build(nc, **aps, out=out)
    result = run(nc, [arrays], core_ids=[0])
    return result.results[0]["out_dram"]
```

```python
from contextlib import ExitStack

import concourse.bass as bass
from concourse import mybir

ALU = mybir.AluOpType
ACT = mybir.ActivationFunctionType
AX = mybir.AxisListType
F32 = mybir.dt.float32
F32R = mybir.dt.float32r
I32 = mybir.dt.int32

FIELDS = 39
DIM = 16
BATCH = 512
SIZE = 128
HALF = SIZE // 2
VOCAB = [12500, 1000, 125000, 12500, 1250, 1250, 1250, 12500, 12500, 125000, 125000, 1250, 125000,
         125000, 125000, 1000, 1000, 1250, 1000, 1250, 1250, 1250, 12500, 12500, 1000, 1000, 12500,
         125000, 12500, 12500, 125000, 1000, 125000, 1250, 12500, 12500, 125000, 125000, 1250]

COLS = 512
ROWS = COLS // DIM
CHUNKS = BATCH // ROWS
PER = 128 // ROWS
GATHERS = -(-FIELDS // PER)
LAST = (FIELDS - PER * (GATHERS - 1)) * ROWS

SHIFTS = 3
PAIR_ROWS = FIELDS * SHIFTS
TILES0 = 7
PARTS0 = [(0, 2), (2, 4), (4, TILES0)]
MIRRORED = range(1, 19)
AGAIN = (SHIFTS * TILES0 - 1) // PER
ARRANGED = FIELDS + AGAIN * PER

TILES = -(-FIELDS // 2)
LAST_TILE = TILES - 1
PIECE = 4
PIECES = TILES // PIECE

GATHERS_AT = {5: 1, 9: 1, 11: 5, 14: 1, 19: 1, 21: 1}
LAG = 2
RING = 6
SPLIT_RING = 5

MODES1 = "FFGVGFGVFG"
MODES0 = "VFFF"
MODES2 = "FFGVGFGVFG"
GROUPS1 = [(1, j, 2, m) for j, m in zip(range(0, TILES, 2), MODES1)]
GROUPS0 = [(0, j, min(2, TILES0 - j), m) for j, m in zip(range(0, TILES0, 2), MODES0)]
GROUPS2 = [(2, j, 2, m) for j, m in zip(range(0, TILES, 2), MODES2)]
START = [(0, j, n, "F") for _, j, n, _ in GROUPS0]
GROUPS = GROUPS1 + GROUPS0 + GROUPS2
N1, N0 = len(GROUPS1), len(GROUPS0)
END1, END0 = N1 - 1, N1 + N0 - 1
LAYER0 = range(N1, N1 + N0)
GROUP_ROWS = {0: PAIR_ROWS, 1: 128, 2: 128}

PROLOGUE, FINAL = 0, CHUNKS


def earlier(g, run=None):
    if run == PROLOGUE:
        return START[:g - N1]
    if run == FINAL and g > END0:
        return START + GROUPS[:N1] + GROUPS[END0 + 1:g]
    return START + GROUPS[:g]


def group_of(g, run=None):
    return START[g - N1] if run == PROLOGUE else GROUPS[g]


def slot(g, run=None):
    return len(earlier(g, run)) % RING


def split_in(modes, groups=GROUPS):
    return sum(m in modes for *_, m in groups)


TOWER_PARTS = [(0, BATCH - ROWS), (BATCH - ROWS, BATCH)]


SPLITS = split_in("VG")
ROUNDS = -(-SPLITS // SPLIT_RING)
SHORT_ROUNDS = ROUNDS * SPLIT_RING - SPLITS
assert SHORT_ROUNDS <= ROUNDS
SPLIT_SLOTS = [q for r in range(ROUNDS) for q in range(SPLIT_RING - (r >= ROUNDS - SHORT_ROUNDS))]


def split_slot(g):
    return SPLIT_SLOTS[split_in("VG", GROUPS[:g])]


def last_use(i, g, run=None):
    here = split_slot(g)
    for b in range(g - 1, -1, -1):
        if GROUPS[b][3] != "F" and not (run == FINAL and b in LAYER0) and split_slot(b) == here:
            return len(earlier(b, run)) + 1
    if isinstance(i, int) and i == 0:
        return None
    for b in range(len(GROUPS) - 1, -1, -1):
        if GROUPS[b][3] != "F" and split_slot(b) == here:
            return len(earlier(b)) + 1 - len(GROUPS)


AFTER1 = END0
AFTER0 = END0 + RING
AFTER2 = RING - 1
AFTER_DIRECT0 = AFTER0 + 2
AFTER_POOL01 = END0 + 8
assert AFTER_POOL01 > END0
assert GROUPS1[-1][3] != "F" and GROUPS2[-1][3] != "F"
assert sum(GATHERS_AT.values()) == GATHERS
assert len(GROUPS) % RING == 0


def build(nc, table, ids, bases, dense, w0, w0_mirror, w1, w2, b0, b1, b2, wt1, bt1, wt2, bt2, wt3, out):
    ctx = ExitStack()

    def sb(name, shape, dt=F32):
        return ctx.enter_context(nc.sbuf_tensor(name, shape, dt))

    def ps(name):
        return ctx.enter_context(nc.psum_tensor(name, [128, COLS], F32))

    def sem(name):
        return ctx.enter_context(nc.semaphore(name))

    with ctx:
        WRITES = 16 * 4
        x_scratch = nc.dram_tensor("x_scratch", [CHUNKS, ARRANGED, COLS], F32, kind="Internal")

        ids_sb = sb("ids_sb", [128, CHUNKS * GATHERS], I32)
        bases_sb = sb("bases_sb", [128, GATHERS], I32)
        rows_now = sb("rows_now", [128, GATHERS], I32)
        gathered_x = sb("gathered_x", [128, GATHERS, DIM])

        w_raw = {0: sb("w0_raw", [PAIR_ROWS, TILES0, SIZE]), 1: sb("w1_raw", [128, TILES, SIZE]),
                 2: sb("w2_raw", [128, TILES, SIZE])}
        mirror = sb("mirror", [PAIR_ROWS, TILES0, SIZE])
        split_tiles, split_list = {}, []
        for layer, j, n, m in GROUPS0 + GROUPS1 + GROUPS2:
            if m != "F":
                split_list.append((layer, j, n - (layer > 0 and j + n == TILES), len(split_tiles)))
                for t in range(j, j + n):
                    split_tiles[layer, t] = len(split_tiles)
        w_hi = sb("w_hi", [128, len(split_tiles), SIZE], F32R)
        w_lo = sb("w_lo", [128, len(split_tiles), SIZE], F32R)
        bias = {0: sb("bias0", [128, 1]), 1: sb("bias1", [128, 1]), 2: sb("bias2", [128, 1])}

        x_pairs = sb("x_pairs", [128, TILES, COLS])
        x_same_in = sb("x_same_in", [PAIR_ROWS, COLS])
        x_shifted = sb("x_shifted", [128, TILES0, COLS])
        direct01 = sb("direct01", [128, COLS])
        direct2 = sb("direct2", [128, COLS])
        z = sb("z", [128, RING, 2, COLS])
        z_hi = sb("z_hi", [128, SPLIT_RING, 2, COLS], F32R)
        z_lo = sb("z_lo", [128, SPLIT_RING, 2, COLS], F32R)

        pooled01 = sb("pooled01", [128, BATCH])
        pooled2 = sb("pooled2", [128, BATCH])
        dense_sb = sb("dense_sb", [DIM, BATCH])
        wt1_sb = sb("wt1_sb", [128, 2, 512])
        wt1_dense = sb("wt1_dense", [DIM, 512])
        wt2_sb = sb("wt2_sb", [128, 4, 256])
        wt3_sb = sb("wt3_sb", [128, 2])
        bt1_sb = sb("bt1_sb", [128, 4])
        bt2_sb = sb("bt2_sb", [128, 2])
        top1 = x_shifted[:, 0:4, :]
        top2 = x_shifted[:, 4:6, :]
        y_sb = sb("y_sb", [1, BATCH])

        acc = {0: ps("acc0"), 1: ps("acc1"), 2: ps("acc2")}
        top_acc0, top_acc1 = ps("top_acc0"), ps("top_acc1")
        y_acc = acc[0][0:1, :]
        x_same = ps("x_same")
        h1 = ps("h1")
        h2 = ps("h2")

        def top_acc(part, m):
            banks = (top_acc0, top_acc1, acc[1], x_same) if part else (top_acc0, top_acc1)
            return banks[m % len(banks)]


        ids_loaded = sem("ids_loaded")
        x_gathered = [sem("x_gathered_first"), sem("x_gathered_rest")]
        scratch_written = sem("scratch_written")
        x_same_loaded = sem("x_same_loaded")
        x_same_ready = sem("x_same_ready")
        x_shifted_loaded = [sem(f"x_shifted_loaded{p}") for p in range(len(PARTS0))]
        x_pairs_loaded = [sem(f"x_pairs_loaded{p}") for p in range(PIECES)]
        w_loaded = {n: sem(f"w{n}_loaded") for n in (0, 1, 2)}
        mirror_loaded = sem("mirror_loaded")
        top_loaded = sem("top_loaded")
        w0_summed = sem("w0_summed")
        w_hi_ready = sem("w_hi_ready")
        w_lo_ready = sem("w_lo_ready")
        mirror_cleared = sem("mirror_cleared")
        z_ready = sem("z_ready")
        z_hi_ready = sem("z_hi_ready")
        z_lo_by_vector = sem("z_lo_by_vector")
        z_lo_by_gpsimd = sem("z_lo_by_gpsimd")
        z_used = sem("z_used")
        h1_ready = sem("h1_ready")
        h2_ready = sem("h2_ready")
        direct0_ready = sem("direct0_ready")
        direct1_ready = sem("direct1_ready")
        direct2_ready = sem("direct2_ready")
        pooled01_ready = sem("pooled01_ready")
        pooled2_ready = sem("pooled2_ready")
        top1_acc_ready = sem("top1_acc_ready")
        top1_ready = sem("top1_ready")
        top2_acc_ready = sem("top2_acc_ready")
        top2_ready = sem("top2_ready")
        y_acc_ready = sem("y_acc_ready")
        y_ready = sem("y_ready")
        out_written = sem("out_written")

        def made(i, g, run=None):
            return i * len(GROUPS) + (len(earlier(g, run)) + 1)

        def split_made(i, g, modes, run=None):
            return i * split_in(modes) + split_in(modes, earlier(g, run) + [GROUPS[g]])


        block = ctx.enter_context(nc.Block())

        @block.sync
        def _(sp):
            def write_scratch(c):
                sp.wait_ge(x_gathered[0], 16 * AGAIN * (c + 1))
                for start in (0, FIELDS):
                    x_c = x_scratch[c, start:start + AGAIN * PER, :].rearrange(
                        "(g f) (r d) -> (f r) g d", f=PER, d=DIM)
                    sp.dma_start(x_c, gathered_x[:, 0:AGAIN, :]).then_inc(scratch_written, 16)
                sp.wait_ge(x_gathered[1], 16 * (GATHERS - AGAIN) * (c + 1))
                whole = PER * (GATHERS - 1)
                x_c = x_scratch[c, AGAIN * PER:whole, :].rearrange("(g f) (r d) -> (f r) g d", f=PER, d=DIM)
                sp.dma_start(x_c, gathered_x[:, AGAIN:GATHERS - 1, :]).then_inc(scratch_written, 16)
                x_c = x_scratch[c, whole:FIELDS, :].rearrange("f (r d) -> (f r) d", d=DIM)
                sp.dma_start(x_c, gathered_x[0:LAST, GATHERS - 1, :]).then_inc(scratch_written, 16)

            def load_layer0(c, written):
                sp.wait_ge(scratch_written, written)
                for k in range(SHIFTS):
                    rows = slice(FIELDS * k, FIELDS * (k + 1))
                    sp.dma_start(x_same_in[rows, :], x_scratch[c, 0:FIELDS, :]).then_inc(x_same_loaded, 16)
                for part, (t0, t1) in enumerate(PARTS0):
                    for k in range(SHIFTS):
                        rows = slice(FIELDS * k, FIELDS * (k + 1))
                        first = x_scratch[c, SHIFTS * t0 + k:SHIFTS * t0 + k + 1, :]
                        src = bass.AP(first.tensor, first.offset,
                                      [[COLS, FIELDS], [SHIFTS * COLS, t1 - t0], [1, COLS]])
                        sp.dma_start(x_shifted[rows, t0:t1, :], src).then_inc(x_shifted_loaded[part], 16)

            def load_pairs(c, p):
                for i in range(2):
                    tiles = PIECE - (i == 1 and p == PIECES - 1)
                    first = x_scratch[c, 2 * PIECE * p + i:2 * PIECE * p + i + 1, :]
                    src = bass.AP(first.tensor, first.offset,
                                  [[0, HALF], [2 * COLS, tiles], [1, COLS]])
                    sp.dma_start(x_pairs[HALF * i:HALF * (i + 1), PIECE * p:PIECE * p + tiles, :], src)\
                        .then_inc(x_pairs_loaded[p], 16)
                if p == PIECES - 1:
                    first = x_scratch[c, FIELDS - 1:FIELDS, :]
                    src = bass.AP(first.tensor, first.offset, [[0, HALF], [1, COLS]])
                    sp.dma_start(x_pairs[HALF:, LAST_TILE, :], src).then_inc(x_pairs_loaded[p], 16)

            sp.dma_start(ids_sb[:, :], ids).then_inc(ids_loaded, 16)
            sp.dma_start(bases_sb[:, :], bases).then_inc(ids_loaded, 16)
            write_scratch(0)
            load_layer0(0, WRITES)
            for p in range(PIECES):
                load_pairs(0, p)
            write_scratch(1)
            sp.wait_ge(z_ready, N0)
            load_layer0(1, 2 * WRITES)

            def iteration(i, ahead):
                for p in range(PIECES):
                    sp.wait_ge(z_ready, made(i, END0 + PIECE // 2 * (p + 1)))
                    load_pairs(i + 1, p)
                if ahead:
                    write_scratch(i + 2)
                    load_layer0(i + 2, i * WRITES + 3 * WRITES)

            with sp.Fori(0, CHUNKS - 2) as i:
                iteration(i, True)
            iteration(CHUNKS - 2, False)
            sp.wait_ge(y_ready, 1)
            sp.dma_start(out.rearrange("b a -> a b"), y_sb[:, :]).then_inc(out_written, 16)
            sp.wait_ge(out_written, 16)

        @block.gpsimd
        def _(pool):
            def find_rows(c):
                nc.gpsimd.tensor_tensor(rows_now[:, :], ids_sb[:, bass.ds(c * GATHERS, GATHERS)],
                                        bases_sb[:, :], ALU.add)
                pool.drain()

            def gather(g):
                n = 128 if g < GATHERS - 1 else LAST
                nc.gpsimd.indirect_dma_start(
                    gathered_x[0:n, g, :], None, table,
                    bass.IndirectOffsetOnAxis(ap=rows_now[0:n, g:g + 1], axis=0)).then_inc(x_gathered[g >= AGAIN], 16)

            def low(i, g, run=None):
                layer, _, n, _ = GROUPS[g]
                s, q = slot(g, run), split_slot(g)
                k = GROUP_ROWS[layer]
                pool.wait_ge(z_hi_ready, split_made(i, g, "VG", run))
                nc.gpsimd.tensor_tensor(z_lo[0:k, q, 0:n, :], z[0:k, s, 0:n, :],
                                        z_hi[0:k, q, 0:n, :].bitcast(F32), ALU.subtract)\
                    .then_inc(z_lo_by_gpsimd, 1)

            mine = [g for g in range(len(GROUPS)) if GROUPS[g][3] == "G"]

            pool.wait_ge(ids_loaded, 32)
            find_rows(0)
            for g in range(GATHERS):
                gather(g)
            pool.wait_ge(scratch_written, WRITES)
            find_rows(1)
            for g in range(GATHERS):
                gather(g)
            with pool.Fori(0, CHUNKS - 2) as i:
                done = 0
                for g in range(len(GROUPS)):
                    if g in GATHERS_AT:
                        if not done:
                            pool.wait_ge(scratch_written, i * WRITES + 2 * WRITES)
                            find_rows(i + 2)
                        for n in range(done, done + GATHERS_AT[g]):
                            gather(n)
                        done += GATHERS_AT[g]
                    if g in mine:
                        low(i, g)
            for g in mine:
                low(CHUNKS - 2, g)
            for g in mine:
                if g not in LAYER0:
                    low(CHUNKS - 1, g, FINAL)

        @block.vector
        def _(dve):
            def product(i, g, run=None):
                layer, j, n, m = group_of(g, run)
                s = slot(g, run)
                k = GROUP_ROWS[layer]
                if not (isinstance(i, int) and made(i, g, run) <= RING):
                    dve.wait_ge(z_used, made(i, g, run) - RING)
                if layer == 0:
                    loads = i * 16 * SHIFTS + 16 * SHIFTS * (1 if run == PROLOGUE else 2)
                    if j == 0:
                        dve.wait_ge(x_same_ready, i + (1 if run == PROLOGUE else 2))
                    for part, (t0, _) in enumerate(PARTS0):
                        if j == t0:
                            dve.wait_ge(x_shifted_loaded[part], loads)
                    in0, h = x_shifted[0:k, j:j + n, :], x_same[0:k, :]
                else:
                    if j % PIECE == 0:
                        loads = 16 * (2 + (j // PIECE == PIECES - 1))
                        dve.wait_ge(x_pairs_loaded[j // PIECE], i * loads + loads)
                    if j == 0:
                        dve.wait_ge({1: h1_ready, 2: h2_ready}[layer], i * 2 + 2)
                    in0, h = x_pairs[:, j:j + n, :], {1: h1, 2: h2}[layer][:, :]
                nc.vector.tensor_tensor(z[0:k, s, 0:n, :], in0, h.unsqueeze(1).broadcast_to([k, n, COLS]),
                                        ALU.mult).then_inc(z_ready, 1)

            def low(i, g, run=None):
                layer, _, n, m = GROUPS[g]
                if m != "V":
                    return
                s, q = slot(g, run), split_slot(g)
                k = GROUP_ROWS[layer]
                dve.wait_ge(z_hi_ready, split_made(i, g, "VG", run))
                nc.vector.tensor_tensor(z_lo[0:k, q, 0:n, :], z[0:k, s, 0:n, :],
                                        z_hi[0:k, q, 0:n, :].bitcast(F32), ALU.subtract)\
                    .then_inc(z_lo_by_vector, 1)

            def pool01(i):
                dve.wait_ge(direct0_ready, i + 1)
                dve.wait_ge(direct1_ready, i + 1)
                nc.vector.tensor_reduce(pooled01[:, bass.ds(i * ROWS, ROWS)],
                                        direct01[:, :].rearrange("p (r d) -> p r d", d=DIM),
                                        AX.X, ALU.add).then_inc(pooled01_ready, 1)

            def pool2(i):
                dve.wait_ge(direct2_ready, i + 1)
                nc.vector.tensor_reduce(pooled2[:, bass.ds(i * ROWS, ROWS)],
                                        direct2[:, :].rearrange("p (r d) -> p r d", d=DIM),
                                        AX.X, ALU.add).then_inc(pooled2_ready, 1)

            def iteration(i, run=None, first=False):
                todo = [g for g in range(len(GROUPS)) if not (run == FINAL and g in LAYER0)]
                owed = []
                for g in todo:
                    if g == END0 + 1:
                        while owed:
                            low(i, owed.pop(0), run)
                        if not first:
                            pool2(i - 1)
                    product(i, g, run)
                    owed.append(g)
                    if len(owed) > LAG:
                        low(i, owed.pop(0), run)
                    if g == AFTER_POOL01:
                        pool01(i)
                while owed:
                    low(i, owed.pop(0), run)

            nc.vector.memset(mirror[:, :, :], 0.0).then_inc(mirror_cleared, 1)
            dve.wait_ge(mirror_loaded, 48)
            dve.wait_ge(w_loaded[0], 32)
            nc.vector.tensor_tensor(w_raw[0][:, :, :], w_raw[0][:, :, :], mirror[:, :, :], ALU.add)\
                .then_inc(w0_summed, 1)
            for n, (layer, t, m, q) in enumerate(split_list):
                k = GROUP_ROWS[layer]
                dve.wait_ge(w_hi_ready, n + 1)
                nc.vector.tensor_tensor(w_lo[0:k, q:q + m, :], w_raw[layer][:, t:t + m, :],
                                        w_hi[0:k, q:q + m, :].bitcast(F32), ALU.subtract).then_inc(w_lo_ready, 1)
            for layer in (1, 2):
                q = split_tiles[layer, LAST_TILE]
                dve.wait_ge(w_hi_ready, len(split_list) + 2 * layer)
                for high_part, low_part, half in ((w_hi, w_lo, slice(0, HALF)), (w_lo, w_hi, slice(HALF, 128))):
                    nc.vector.tensor_tensor(low_part[half, q, :], w_raw[layer][half, LAST_TILE, :],
                                            high_part[half, q, :].bitcast(F32), ALU.subtract)\
                        .then_inc(w_lo_ready, 1)
            for g in LAYER0:
                product(0, g, PROLOGUE)
            iteration(0, first=True)
            with dve.Fori(1, CHUNKS - 1) as i:
                iteration(i)
            iteration(CHUNKS - 1, FINAL)
            pool2(CHUNKS - 1)
            dve.wait_ge(y_acc_ready, len(TOWER_PARTS))
            nc.vector.tensor_copy(y_sb[:, :], y_acc).then_inc(y_ready, 1)

        @block.scalar
        def _(act):
            def high(i, g, run=None):
                layer, _, n, m = GROUPS[g]
                if m == "F":
                    return
                s, q = slot(g, run), split_slot(g)
                k = GROUP_ROWS[layer]
                if last_use(i, g, run) is not None:
                    act.wait_ge(z_used, i * len(GROUPS) + last_use(i, g, run))
                act.wait_ge(z_ready, made(i, g, run))
                nc.scalar.activation(z_hi[0:k, q, 0:n, :], z[0:k, s, 0:n, :], ACT.Copy)\
                    .then_inc(z_hi_ready, 1)

            def place_same(n):
                act.wait_ge(x_same_loaded, n * 16 * SHIFTS + 16 * SHIFTS)
                nc.scalar.activation(x_same[0:PAIR_ROWS, :], x_same_in[:, :], ACT.Copy).then_inc(x_same_ready, 1)

            def relu(dst, layer, p0, done):
                nc.scalar.activation(dst, acc[layer][p0:p0 + HALF, :], ACT.Relu,
                                     bias=bias[layer][p0:p0 + HALF, :]).then_inc(done, 1)

            def finish0(c):
                act.wait_ge(z_used, made(0, END0, PROLOGUE) if isinstance(c, int) and c == 0 else
                            made(c - 1, END0))
                relu(h1[0:HALF, :], 0, 0, h1_ready)
                relu(h1[HALF:, :], 0, 0, h1_ready)

            def finish0_direct(c, first=False):
                if not first:
                    act.wait_ge(pooled01_ready, c)
                relu(direct01[HALF:, :], 0, HALF, direct0_ready)

            def finish1(c):
                act.wait_ge(z_used, made(c, END1))
                relu(h2[HALF:, :], 1, HALF, h2_ready)
                relu(h2[0:HALF, :], 1, HALF, h2_ready)
                relu(direct01[0:HALF, :], 1, 0, direct1_ready)

            def finish2(c, run=None):
                act.wait_ge(z_used, made(c, len(GROUPS) - 1, run))
                nc.scalar.activation(direct2[:, :], acc[2][:, :], ACT.Relu, bias=bias[2][:, :])\
                    .then_inc(direct2_ready, 1)

            def tower_relus(part):
                b0, b1 = TOWER_PARTS[part]
                for m in range(4):
                    act.wait_ge(top1_acc_ready, 4 * part + m + 1)
                    nc.scalar.activation(top1[:, m, b0:b1], top_acc(part, m)[:, b0:b1], ACT.Relu,
                                         bias=bt1_sb[:, m:m + 1]).then_inc(top1_ready, 1)
                for m in range(2):
                    act.wait_ge(top2_acc_ready, 2 * part + m + 1)
                    nc.scalar.activation(top2[:, m, b0:b1], top_acc(part, m)[:, b0:b1], ACT.Relu,
                                         bias=bt2_sb[:, m:m + 1]).then_inc(top2_ready, 1)

            def iteration(i, run=None, first=False):
                for g in range(len(GROUPS)):
                    if run == FINAL and g in LAYER0:
                        continue
                    high(i, g, run)
                    if g == AFTER2 and not first:
                        finish2(i - 1)
                    if g == 5 and run != FINAL:
                        place_same(i + 1)
                    if g == (END1 if run == FINAL else AFTER1):
                        finish1(i)
                        if run == FINAL:
                            act.wait_ge(top_loaded, 16 * 7)
                            tower_relus(0)
                    if g == AFTER0 and run != FINAL:
                        finish0(i + 1)
                    if g == AFTER_DIRECT0 and run != FINAL:
                        finish0_direct(i + 1)

            act.wait_ge(ids_loaded, 32)
            act.dma_start(w_raw[0][:, :, :], w0).then_inc(w_loaded[0], 16)
            act.wait_ge(mirror_cleared, 1)
            for k, t0, t1 in ((0, 1, 7), (1, 0, 6), (2, 0, 6)):
                rows = slice(FIELDS * k, FIELDS * (k + 1))
                act.dma_start(mirror[rows, t0:t1, :], w0_mirror[rows, t0:t1, :])\
                    .then_inc(mirror_loaded, 16)
            for n, b in ((0, b0), (1, b1), (2, b2)):
                act.dma_start(bias[n][:, :], b.rearrange("(p a) -> p a", a=1)).then_inc(w_loaded[n], 16)
            for n, w in ((1, w1), (2, w2)):
                whole = FIELDS // 2
                act.dma_start(w_raw[n][:, 0:whole, :],
                              w[0:128 * whole, :].rearrange("(t p) s -> p t s", p=128)).then_inc(w_loaded[n], 16)
                for half in (slice(0, HALF), slice(HALF, 128)):
                    act.dma_start(w_raw[n][half, LAST_TILE, :], w[128 * whole:, :]).then_inc(w_loaded[n], 16)
            act.dma_start(wt1_sb[:, :, :], wt1[0:256, :].rearrange("(t p) n -> p t n", p=128)).then_inc(top_loaded, 16)
            act.dma_start(wt1_dense[:, :], wt1[256:, :]).then_inc(top_loaded, 16)
            act.dma_start(wt2_sb[:, :, :], wt2.rearrange("(t p) n -> p t n", p=128)).then_inc(top_loaded, 16)
            act.dma_start(wt3_sb[:, :], wt3).then_inc(top_loaded, 16)
            act.dma_start(bt1_sb[:, :], bt1).then_inc(top_loaded, 16)
            act.dma_start(bt2_sb[:, :], bt2).then_inc(top_loaded, 16)
            act.dma_start(dense_sb[:, :], dense).then_inc(top_loaded, 16)
            act.wait_ge(w0_summed, 1)
            for n, (layer, t, m, q) in enumerate(split_list):
                k = GROUP_ROWS[layer]
                if layer and split_list[n - 1][0] != layer:
                    act.wait_ge(w_loaded[layer], 64)
                nc.scalar.activation(w_hi[0:k, q:q + m, :], w_raw[layer][:, t:t + m, :], ACT.Copy)\
                    .then_inc(w_hi_ready, 1)
            for layer in (1, 2):
                q = split_tiles[layer, LAST_TILE]
                for stack, half in ((w_hi, slice(0, HALF)), (w_lo, slice(HALF, 128))):
                    nc.scalar.activation(stack[half, q, :], w_raw[layer][half, LAST_TILE, :], ACT.Copy)\
                        .then_inc(w_hi_ready, 1)
            place_same(0)
            finish0(0)
            finish0_direct(0, first=True)
            iteration(0, first=True)
            with act.Fori(1, CHUNKS - 1) as i:
                iteration(i)
            iteration(CHUNKS - 1, FINAL)
            finish2(CHUNKS - 1, FINAL)
            tower_relus(1)

        @block.tensor
        def _(pe):
            def group(i, g, run=None):
                layer, j, n, m = group_of(g, run)
                s = slot(g, run)
                k = GROUP_ROWS[layer]
                tiles = TILES if layer else TILES0
                if m == "F":
                    pe.wait_ge(z_ready, made(i, g, run))
                else:
                    lo_ready = {"V": z_lo_by_vector, "G": z_lo_by_gpsimd}[m]
                    pe.wait_ge(lo_ready, split_made(i, g, m, run))
                for t in range(j, j + n):
                    if m == "F":
                        parts = [(w_raw[layer][:, t, :], z[0:k, s, t - j, :])]
                    else:
                        q, r = split_tiles[layer, t], split_slot(g)
                        hi, lo = z_hi[0:k, r, t - j, :], z_lo[0:k, r, t - j, :]
                        parts = [(w_lo[0:k, q, :], hi), (w_hi[0:k, q, :], hi), (w_hi[0:k, q, :], lo)]
                        if layer and t == LAST_TILE:
                            parts = [(w_lo[:, q, :], hi), (w_hi[:, q, :], lo)]
                    for u, (w, of) in enumerate(parts):
                        last = nc.tensor.matmul(acc[layer][:, :], w, of,
                                                start=(t == 0 and u == 0),
                                                stop=(t == tiles - 1 and u == len(parts) - 1))
                last.then_inc(z_used, 1)

            def tower(part):
                b0, b1 = TOWER_PARTS[part]
                pe.wait_ge(top_loaded, 16 * 7)
                pe.wait_ge(pooled01_ready, b1 // ROWS)
                if part:
                    pe.wait_ge(top2_ready, 2 * part)

                def without_layer2(m):
                    at = slice(128 * m, 128 * (m + 1))
                    a = top_acc(part, m)[:, b0:b1]
                    nc.tensor.matmul(a, wt1_sb[:, 0, at], pooled01[:, b0:b1], start=True, stop=False)
                    nc.tensor.matmul(a, wt1_dense[:, at], dense_sb[:, b0:b1], start=False, stop=False)

                def add_layer2(m):
                    nc.tensor.matmul(top_acc(part, m)[:, b0:b1], wt1_sb[:, 1, 128 * m:128 * (m + 1)],
                                     pooled2[:, b0:b1], start=False, stop=True).then_inc(top1_acc_ready, 1)

                if part:
                    for m in range(4):
                        without_layer2(m)
                    pe.wait_ge(pooled2_ready, b1 // ROWS)
                    for m in range(4):
                        add_layer2(m)
                else:
                    pe.wait_ge(pooled2_ready, b1 // ROWS)
                    for m in range(4):
                        if m >= 2:
                            pe.wait_ge(top1_ready, m - 1)
                        without_layer2(m)
                        add_layer2(m)
                pe.wait_ge(top1_ready, 4 * part + 4)
                for m in range(2):
                    for t in range(4):
                        last = nc.tensor.matmul(top_acc(part, m)[:, b0:b1], wt2_sb[:, t, 128 * m:128 * (m + 1)],
                                                top1[:, t, b0:b1], start=(t == 0), stop=(t == 3))
                    last.then_inc(top2_acc_ready, 1)
                for m in range(2):
                    pe.wait_ge(top2_ready, 2 * part + m + 1)
                    last = nc.tensor.matmul(y_acc[:, b0:b1], wt3_sb[:, m:m + 1], top2[:, m, b0:b1],
                                            start=(m == 0), stop=(m == 1))
                last.then_inc(y_acc_ready, 1)

            def iteration(i, run=None):
                for g in range(len(GROUPS)):
                    layer = GROUPS[g][0]
                    if run == FINAL and g == END0 + 1:
                        tower(0)
                    if run == FINAL and layer == 0:
                        continue
                    if g == N1:
                        pe.wait_ge(h1_ready, i * 2 + 2)
                        pe.wait_ge(direct0_ready, i + 1)
                    group(i, g, run)

            pe.wait_ge(w0_summed, 1)
            for g in LAYER0:
                group(0, g, PROLOGUE)
            pe.wait_ge(w_loaded[1], 64)
            pe.wait_ge(w_loaded[2], 64)
            pe.wait_ge(w_lo_ready, len(split_list) + 4)
            with pe.Fori(0, CHUNKS - 1) as i:
                iteration(i)
            iteration(CHUNKS - 1, FINAL)
            tower(1)


def kernel(**inputs):
    import numpy as np
    import concourse.bacc as bacc
    from concourse import mybir as mb
    from concourse.bass_utils import run_bass_kernel_spmd as run

    a = {k: np.asarray(v) for k, v in inputs.items()}
    table = np.concatenate([a[f"tbl_{f}"] for f in range(FIELDS)])
    starts = np.concatenate([[0], np.cumsum(VOCAB)[:-1]]).astype(np.int32)
    padded = np.zeros((BATCH, GATHERS * PER), a["ids"].dtype)
    padded[:, :FIELDS] = a["ids"]
    ids = padded.reshape(CHUNKS, ROWS, GATHERS, PER).transpose(3, 1, 0, 2).reshape(128, CHUNKS * GATHERS)
    bases = np.zeros(GATHERS * PER, np.int32)
    bases[:FIELDS] = starts
    bases = np.repeat(bases.reshape(GATHERS, PER).T, ROWS, axis=0)
    r = a["L0_rec_W0"].reshape(FIELDS, FIELDS, SIZE)
    f = np.arange(FIELDS)[None, :, None]
    s = SHIFTS * np.arange(TILES0)[None, None, :] + np.arange(SHIFTS)[:, None, None]
    other = (f + s) % FIELDS
    w0 = r[f, other].reshape(PAIR_ROWS, TILES0, SIZE)
    w0_mirror = r[other, f].reshape(PAIR_ROWS, TILES0, SIZE)
    swap = np.r_[HALF:SIZE, 0:HALF]
    wt1 = a["W_top1"][np.r_[HALF:SIZE, 0:HALF, SIZE:272]]
    given = {
        "table": table, "ids": ids, "bases": bases, "dense": a["dense_ctx"].T,
        "w0": w0, "w0_mirror": w0_mirror, "w1": a["L0_rec_W1"][:, swap], "w2": a["L0_rec_W2"],
        "b0": a["L0_rec_b0"], "b1": a["L0_rec_b1"][swap], "b2": a["L0_rec_b2"],
        "wt1": wt1, "bt1": a["b_top1"].reshape(4, 128).T, "wt2": a["W_top2"],
        "bt2": a["b_top2"].reshape(2, 128).T, "wt3": a["W_top3"].reshape(2, 128).T,
    }
    nc = bacc.Bacc("TRN2", target_bir_lowering=False, num_devices=1)
    arrays, aps = {}, {}
    for name, x in given.items():
        x = np.ascontiguousarray(x)
        arrays[name + "_dram"] = x
        aps[name] = nc.dram_tensor(name + "_dram", x.shape, mb.dt.from_np(x.dtype), kind="ExternalInput").ap()
    out = nc.dram_tensor("out_dram", (BATCH, 1), mb.dt.float32, kind="ExternalOutput").ap()
    build(nc, **aps, out=out)
    result = run(nc, [arrays], core_ids=[0])
    return result.results[0]["out_dram"]
```
